# Optimizing a Trainium2 kernel written in Bass

```python
import numpy as np
import jax
import jax.numpy as jnp

def _softmax(x, axis=-1):
    return jax.nn.softmax(x, axis=axis)

def _gelu(x):
    return jax.nn.gelu(x, approximate=True)

def _silu(x):
    return jax.nn.silu(x)

def _sigmoid(x):
    return jax.nn.sigmoid(x)

def _layernorm(x, axis=-1, eps=1e-05):
    m = jnp.mean(x, axis=axis, keepdims=True)
    v = jnp.var(x, axis=axis, keepdims=True)
    return (x - m) / jnp.sqrt(v + eps)

def _scatter_add(tgt, idx, src, axis=0):
    return tgt.at[idx].add(src)

def _segment_sum(src, seg, n):
    return jax.ops.segment_sum(src, seg, n)
kernel_name = 'mk_macaron_d1_jaxref_r8_78e441'

def setup_inputs(seed: int=0):
    np.random.seed(seed)
    _w = jnp.asarray

    def _L0_attn_setup():
        import jax, jax.numpy as jnp
        import numpy as np
        B, L = (2, 128)
        D_MODEL, D_CKV, D_CQ = (128, 32, 64)
        N_HEAD, D_HEAD, D_ROPE = (8, 64, 32)
        N_IDX_HEAD = 4
        K_TS, LW = (96, 64)
        ROPE_BASE = 10000.0

        def _pope(x, angles):
            cos, sin = (jnp.cos(angles), jnp.sin(angles))
            mu1, mu2 = jnp.split(jax.nn.softplus(x), 2, axis=-1)
            return jnp.concatenate([mu1 * cos - mu2 * sin, mu1 * sin + mu2 * cos], axis=-1)

        def _forward(x, W_dkv, W_uk, W_uv, W_dq, W_uq, W_qr, W_kr, W_out, idx_wq, idx_wk, idx_w, raw_delta):
            B_, L_, _ = x.shape
            c_kv = x @ W_dkv
            q_i = (x @ idx_wq).reshape(B_, L_, N_IDX_HEAD, D_HEAD)
            k_i = x @ idx_wk
            s_i = jax.nn.relu(jnp.einsum('bthd,bsd->bths', q_i, k_i))
            I = jnp.einsum('bths,h->bts', s_i, idx_w)
            qpos = jnp.arange(L_)[:, None]
            kpos = jnp.arange(L_)[None, :]
            local = (kpos >= qpos - LW + 1) & (kpos <= qpos)
            causal = kpos > qpos
            I = jnp.where(local[None], jnp.inf, I)
            I = jnp.where(causal[None], -jnp.inf, I)
            kk = min(K_TS, L_)
            _, idx = jax.lax.top_k(I, kk)
            bi = jnp.arange(B_)[:, None, None]
            key_c = (c_kv @ W_uk)[bi, idx].reshape(B_, L_, kk, N_HEAD, D_HEAD)
            value = (c_kv @ W_uv)[bi, idx].reshape(B_, L_, kk, N_HEAD, D_HEAD)
            c_q = x @ W_dq
            query_c = (c_q @ W_uq).reshape(B_, L_, N_HEAD, D_HEAD)
            half = D_ROPE // 2
            theta = 1.0 / ROPE_BASE ** (2.0 * jnp.arange(half, dtype=jnp.float32) / D_ROPE)
            delta = -2.0 * jnp.pi * jax.nn.sigmoid(raw_delta)
            angles_q = jnp.arange(L_, dtype=jnp.float32)[:, None] * theta[None, :] + delta
            query_r = _pope((c_q @ W_qr).reshape(B_, L_, N_HEAD, D_ROPE), angles_q[None, :, None, :])
            kr_sel = (x @ W_kr)[bi, idx]
            angles_k = jnp.arange(kk, dtype=jnp.float32)[:, None] * theta[None, :] + delta
            key_r = _pope(kr_sel, angles_k[None, None, :, :])
            scale = (D_HEAD + D_ROPE) ** (-0.5)
            q_c = query_c.transpose(0, 2, 1, 3)
            q_r = query_r.transpose(0, 2, 1, 3)
            k_c = key_c.transpose(0, 3, 1, 2, 4)
            v = value.transpose(0, 3, 1, 2, 4)
            scores = (jnp.einsum('bhld,bhlkd->bhlk', q_c, k_c) + jnp.einsum('bhld,blkd->bhlk', q_r, key_r)) * scale
            attn = jax.nn.softmax(scores.astype(jnp.float32), axis=-1).astype(v.dtype)
            out = jnp.einsum('bhlk,bhlkd->bhld', attn, v)
            out = out.transpose(0, 2, 1, 3).reshape(B_, L_, N_HEAD * D_HEAD)
            return out @ W_out
        key = jax.random.key(seed)
        ks = jax.random.split(key, 14)

        def w(k, shape, fan_in):
            return jax.random.normal(k, shape, dtype=jnp.float32) * fan_in ** (-0.5)
        return {'x': jax.random.normal(ks[0], (B, L, D_MODEL), dtype=jnp.float32), 'W_dkv': w(ks[1], (D_MODEL, D_CKV), D_MODEL), 'W_uk': w(ks[2], (D_CKV, N_HEAD * D_HEAD), D_CKV), 'W_uv': w(ks[3], (D_CKV, N_HEAD * D_HEAD), D_CKV), 'W_dq': w(ks[4], (D_MODEL, D_CQ), D_MODEL), 'W_uq': w(ks[5], (D_CQ, N_HEAD * D_HEAD), D_CQ), 'W_qr': w(ks[6], (D_CQ, N_HEAD * D_ROPE), D_CQ), 'W_kr': w(ks[7], (D_MODEL, D_ROPE), D_MODEL), 'W_out': w(ks[8], (N_HEAD * D_HEAD, D_MODEL), N_HEAD * D_HEAD), 'idx_wq': w(ks[9], (D_MODEL, N_IDX_HEAD * D_HEAD), D_MODEL), 'idx_wk': w(ks[10], (D_MODEL, D_HEAD), D_MODEL), 'idx_w': jnp.ones((N_IDX_HEAD,), dtype=jnp.float32), 'raw_delta': jax.random.normal(ks[11], (D_ROPE // 2,), dtype=jnp.float32) * 0.1}
    _L0_attn_in = _L0_attn_setup()

    def _L0_ffn_setup():
        import jax, jax.numpy as jnp
        import numpy as np
        DIM = 128
        HIDDEN = 384
        SCALE = 1.0 / 127.0

        def _dequant(w_int, dtype):
            return w_int.astype(dtype) * jnp.asarray(SCALE, dtype)
        key = jax.random.key(seed)
        k_x, k_g, k_u, k_d = jax.random.split(key, 4)
        x = jax.random.normal(k_x, (4, 256, DIM), dtype=jnp.float32)
        w_gate = jax.random.randint(k_g, (HIDDEN, DIM), -127, 128, dtype=jnp.int32)
        w_up = jax.random.randint(k_u, (HIDDEN, DIM), -127, 128, dtype=jnp.int32)
        w_down = jax.random.randint(k_d, (DIM, HIDDEN), -127, 128, dtype=jnp.int32)
        return {'x': x, 'w_gate': w_gate, 'w_up': w_up, 'w_down': w_down}
    _L0_ffn_in = _L0_ffn_setup()
    _d = {'L0_attn_x': _L0_attn_in['x'], 'L0_attn_W_dkv': _L0_attn_in['W_dkv'], 'L0_attn_W_uk': _L0_attn_in['W_uk'], 'L0_attn_W_uv': _L0_attn_in['W_uv'], 'L0_attn_W_dq': _L0_attn_in['W_dq'], 'L0_attn_W_uq': _L0_attn_in['W_uq'], 'L0_attn_W_qr': _L0_attn_in['W_qr'], 'L0_attn_W_kr': _L0_attn_in['W_kr'], 'L0_attn_W_out': _L0_attn_in['W_out'], 'L0_attn_idx_wq': _L0_attn_in['idx_wq'], 'L0_attn_idx_wk': _L0_attn_in['idx_wk'], 'L0_attn_idx_w': _L0_attn_in['idx_w'], 'L0_attn_raw_delta': _L0_attn_in['raw_delta'], 'L0_ffn_w_gate': _L0_ffn_in['w_gate'], 'L0_ffn_w_up': _L0_ffn_in['w_up'], 'L0_ffn_w_down': _L0_ffn_in['w_down']}
    _x0 = _d['L0_attn_x']
    _d['L0_attn_x'] = jax.random.normal(jax.random.fold_in(jax.random.key(seed), 1), (2, 1024, 128), dtype=_x0.dtype)
    del _x0
    return _d

def reference(L0_attn_x, L0_attn_W_dkv, L0_attn_W_uk, L0_attn_W_uv, L0_attn_W_dq, L0_attn_W_uq, L0_attn_W_qr, L0_attn_W_kr, L0_attn_W_out, L0_attn_idx_wq, L0_attn_idx_wk, L0_attn_idx_w, L0_attn_raw_delta, L0_ffn_w_gate, L0_ffn_w_up, L0_ffn_w_down):

    def _L0_attn_ref(x, W_dkv, W_uk, W_uv, W_dq, W_uq, W_qr, W_kr, W_out, idx_wq, idx_wk, idx_w, raw_delta):
        import jax, jax.numpy as jnp
        import numpy as np
        B, L = (2, 128)
        D_MODEL, D_CKV, D_CQ = (128, 32, 64)
        N_HEAD, D_HEAD, D_ROPE = (8, 64, 32)
        N_IDX_HEAD = 4
        K_TS, LW = (96, 64)
        ROPE_BASE = 10000.0

        def _pope(x, angles):
            cos, sin = (jnp.cos(angles), jnp.sin(angles))
            mu1, mu2 = jnp.split(jax.nn.softplus(x), 2, axis=-1)
            return jnp.concatenate([mu1 * cos - mu2 * sin, mu1 * sin + mu2 * cos], axis=-1)

        def _forward(x, W_dkv, W_uk, W_uv, W_dq, W_uq, W_qr, W_kr, W_out, idx_wq, idx_wk, idx_w, raw_delta):
            B_, L_, _ = x.shape
            c_kv = x @ W_dkv
            q_i = (x @ idx_wq).reshape(B_, L_, N_IDX_HEAD, D_HEAD)
            k_i = x @ idx_wk
            s_i = jax.nn.relu(jnp.einsum('bthd,bsd->bths', q_i, k_i))
            I = jnp.einsum('bths,h->bts', s_i, idx_w)
            qpos = jnp.arange(L_)[:, None]
            kpos = jnp.arange(L_)[None, :]
            local = (kpos >= qpos - LW + 1) & (kpos <= qpos)
            causal = kpos > qpos
            I = jnp.where(local[None], jnp.inf, I)
            I = jnp.where(causal[None], -jnp.inf, I)
            kk = min(K_TS, L_)
            _, idx = jax.lax.top_k(I, kk)
            bi = jnp.arange(B_)[:, None, None]
            key_c = (c_kv @ W_uk)[bi, idx].reshape(B_, L_, kk, N_HEAD, D_HEAD)
            value = (c_kv @ W_uv)[bi, idx].reshape(B_, L_, kk, N_HEAD, D_HEAD)
            c_q = x @ W_dq
            query_c = (c_q @ W_uq).reshape(B_, L_, N_HEAD, D_HEAD)
            half = D_ROPE // 2
            theta = 1.0 / ROPE_BASE ** (2.0 * jnp.arange(half, dtype=jnp.float32) / D_ROPE)
            delta = -2.0 * jnp.pi * jax.nn.sigmoid(raw_delta)
            angles_q = jnp.arange(L_, dtype=jnp.float32)[:, None] * theta[None, :] + delta
            query_r = _pope((c_q @ W_qr).reshape(B_, L_, N_HEAD, D_ROPE), angles_q[None, :, None, :])
            kr_sel = (x @ W_kr)[bi, idx]
            angles_k = jnp.arange(kk, dtype=jnp.float32)[:, None] * theta[None, :] + delta
            key_r = _pope(kr_sel, angles_k[None, None, :, :])
            scale = (D_HEAD + D_ROPE) ** (-0.5)
            q_c = query_c.transpose(0, 2, 1, 3)
            q_r = query_r.transpose(0, 2, 1, 3)
            k_c = key_c.transpose(0, 3, 1, 2, 4)
            v = value.transpose(0, 3, 1, 2, 4)
            scores = (jnp.einsum('bhld,bhlkd->bhlk', q_c, k_c) + jnp.einsum('bhld,blkd->bhlk', q_r, key_r)) * scale
            attn = jax.nn.softmax(scores.astype(jnp.float32), axis=-1).astype(v.dtype)
            out = jnp.einsum('bhlk,bhlkd->bhld', attn, v)
            out = out.transpose(0, 2, 1, 3).reshape(B_, L_, N_HEAD * D_HEAD)
            return out @ W_out
        return _forward(x, W_dkv, W_uk, W_uv, W_dq, W_uq, W_qr, W_kr, W_out, idx_wq, idx_wk, idx_w, raw_delta)

    def _L0_ffn_ref(x, w_gate, w_up, w_down):
        import jax, jax.numpy as jnp
        import numpy as np
        DIM = 128
        HIDDEN = 384
        SCALE = 1.0 / 127.0

        def _dequant(w_int, dtype):
            return w_int.astype(dtype) * jnp.asarray(SCALE, dtype)
        wg = _dequant(w_gate, x.dtype)
        wu = _dequant(w_up, x.dtype)
        wd = _dequant(w_down, x.dtype)
        gate = jnp.einsum('bsd,hd->bsh', x, wg)
        up = jnp.einsum('bsd,hd->bsh', x, wu)
        h = jax.nn.silu(gate) * up
        return jnp.einsum('bsh,dh->bsd', h, wd)
    x = L0_attn_x
    x = x + 0.5 * _L0_ffn_ref(_layernorm(x, axis=-1), L0_ffn_w_gate, L0_ffn_w_up, L0_ffn_w_down)
    x = x + _L0_attn_ref(_layernorm(x, axis=-1), L0_attn_W_dkv, L0_attn_W_uk, L0_attn_W_uv, L0_attn_W_dq, L0_attn_W_uq, L0_attn_W_qr, L0_attn_W_kr, L0_attn_W_out, L0_attn_idx_wq, L0_attn_idx_wk, L0_attn_idx_w, L0_attn_raw_delta)
    x = x + 0.5 * _L0_ffn_ref(_layernorm(x, axis=-1), L0_ffn_w_gate, L0_ffn_w_up, L0_ffn_w_down)
    return x

_drawn_inputs = setup_inputs


def setup_inputs(seed=0):
    import zlib

    import numpy as np

    out = dict(_drawn_inputs(seed))
    spreads = {'L0_attn_idx_w': (1.0, 0.6)}
    factors = {'L0_attn_W_dkv': 8.0,
     'L0_attn_W_uk': 8.0,
     'L0_attn_W_uv': 8.0,
     'L0_attn_W_dq': 8.0,
     'L0_attn_W_uq': 8.0,
     'L0_attn_W_qr': 8.0,
     'L0_attn_W_kr': 8.0,
     'L0_attn_W_out': 8.0,
     'L0_attn_idx_wq': 8.0,
     'L0_attn_idx_wk': 8.0,
     'L0_attn_raw_delta': 8.0}
    for name, (base, spread) in spreads.items():
        noise = np.random.default_rng([zlib.crc32(name.encode()), seed]).standard_normal(out[name].shape)
        drawn = base * np.exp(spread * noise) if base else spread * noise
        out[name] = jnp.asarray(drawn.astype(out[name].dtype))
    for name, factor in factors.items():
        out[name] = (out[name] * factor).astype(out[name].dtype)
    return out
```

```python
from contextlib import ExitStack

import numpy as np

import concourse.bass as bass
from concourse import mybir

ALU = mybir.AluOpType
ACT = mybir.ActivationFunctionType
F32 = mybir.dt.float32
I32 = mybir.dt.int32
U32 = mybir.dt.uint32

P = 128
BATCH, LEN = 2, 1024
D = 128
HID = 384
HC = HID // P
NH, DH = 8, 64
DC, DR, DQ = 32, 32, 64
HALF = DR // 2
NI = 4
TOPK, LW = 96, 64
SEL = TOPK - LW
KD = DC + DR

TPB = LEN // P
TILES = BATCH * TPB
RING = 4
WIN = 80
GROUP = P // SEL
QUAD = 16
NG = P // GROUP
DUO = 2 * QUAD
ND = P // DUO
SC = SEL * GROUP
SW = SC + WIN
ICOLS = LEN - LW
SCALE = float(KD + DR) ** -0.5
WSCALE = 1.0 / 127.0
NEG = -1.0e30
FUTURE = -1.0e38
TAKEN = -3.0e38
EPS = 1e-5
NTRIG = 2 * TPB + 1
RANKS = 2 * TPB

C_ID = 0
C_MS = C_ID + P
C_MS0 = C_MS + SW
C_M1 = C_MS0 + SW
C_M0 = C_M1 + P
C_COS = C_M0 + TOPK
C_SIN = C_COS + NTRIG * HALF
C_END = C_SIN + NTRIG * HALF


def shape_constants():
    c = np.zeros((P, C_END), np.float32)
    c[:, C_ID:C_ID + P] = np.eye(P)
    row = np.arange(P)
    t16 = row // NH
    col = np.arange(SC)
    diag = (t16[:, None] % GROUP) == (col[None, :] // SEL)
    w = np.arange(WIN)
    inside = (w[None, :] >= t16[:, None] + 1) & (w[None, :] <= t16[:, None] + LW)
    c[:, C_MS:C_MS + SC] = np.where(diag, 0.0, NEG)
    c[:, C_MS + SC:C_MS + SW] = np.where(inside, 0.0, NEG)
    c[:, C_MS0:C_MS0 + SC] = np.where(diag, 0.0, NEG)
    c[:, C_MS0 + SC:C_MS0 + SW] = np.where(w[None, :] < LW, 0.0, NEG) + np.zeros((P, 1))
    t = GROUP * (row % NG) + row // NG
    s = np.arange(P)
    c[:, C_M1:C_M1 + P] = np.where(s[None, :] > t[:, None], TAKEN, 0.0)
    te = np.maximum(t, LW - 1)[:, None]
    s = np.arange(TOPK)[None, :]
    c[:, C_M0:C_M0 + TOPK] = np.where(s > te, FUTURE, np.where(s > te - LW, TAKEN, 0.0))
    theta = (1.0 / np.float32(10000.0) ** (np.float32(2.0) * np.arange(HALF, dtype=np.float32) / np.float32(DR))).astype(np.float32)
    pos = [P * i + row for i in range(TPB)]
    pos += [p + np.maximum(p, LW - 1) - (LW - 1) for p in pos]
    pos += [LW + row % SEL]
    angle = (np.stack(pos, 1).astype(np.float32)[:, :, None] * theta).astype(np.float64)
    c[:, C_COS:C_SIN] = np.cos(angle).reshape(P, -1)
    c[:, C_SIN:C_END] = np.sin(angle).reshape(P, -1)
    return c


AHEAD1, AHEAD, BEHIND = 3, 2, -1
STEP = [
    ("value", -1), ("normm", AHEAD), ("turn", 0), ("stat1", AHEAD1), ("proj", AHEAD), ("score", 1),
    ("norm1", AHEAD1), ("key", 2), ("krow", AHEAD),
    ("value", 0), ("index", AHEAD), ("turn", 1), ("gate1", AHEAD1), ("score", 2), ("act1", AHEAD1), ("key", 3),
    ("hid1", AHEAD1),
    ("value", 1), ("pick0", AHEAD), ("turn", 2), ("mix", BEHIND), ("query", AHEAD), ("score", 3),
    ("pick1", AHEAD), ("norm2", BEHIND), ("key", 4), ("gate2", BEHIND), ("rope", AHEAD),
    ("value", 2), ("pick2", AHEAD), ("turn", 3), ("act2", BEHIND), ("keysT", AHEAD), ("score", 4),
    ("pick3", AHEAD), ("hid2", BEHIND), ("cwin", AHEAD), ("key", 5), ("queryT", AHEAD), ("store", BEHIND)]
BY_DUO = ("key", "score", "turn", "value")


def run_steps(parts, setup=None):
    for n in range(-AHEAD1, TILES - BEHIND):
        for part, ahead in STEP:
            duo = part in BY_DUO
            at = (ND * n if duo else n) + ahead
            if n == -AHEAD and part == "index" and setup:
                setup()
            if part in parts and 0 <= at < (ND * TILES if duo else TILES):
                if duo:
                    parts[part](at // ND, at % ND)
                else:
                    parts[part](at)



def columns(n):
    i = n % TPB
    return TOPK if i == 0 else P * i + LW


def slot(g):
    d, q, k = g // (2 * GROUP), g // GROUP % 2, g % GROUP
    return 2 * GROUP * d + 2 * k + q


def chunks(n):
    w = columns(n)
    return [(a, min(512, w - a)) for a in range(0, w, 512)]


def fills(n):
    return NI * len(chunks(n))


def fills_before(n):
    return sum(fills(m) for m in range(n))


def macaron_block(nc, x, w_dkv, w_uk, w_uv, w_dq, w_uq, w_qr, w_kr, w_out, iwq, iwk, iw, raw_delta,
                  w_gate, w_up, w_down, consts, out):
    with ExitStack() as ctx:
        def sb(name, shape, dt=F32):
            return ctx.enter_context(nc.sbuf_tensor(name, shape, dt))

        def bank(name):
            return ctx.enter_context(nc.psum_tensor(name, [P, 512], F32))

        def sem(name):
            return ctx.enter_context(nc.semaphore(name))

        table = nc.dram_tensor("key_table", [BATCH * LEN, KD], F32).ap()

        ps_f1, ps_f2, ps_i0, ps_i1, ps_tk, ps_tp = [
            bank(m) for m in ("ps_f1", "ps_f2", "ps_i0", "ps_i1", "ps_tk", "ps_tp")]
        ps_i = (ps_i0, ps_i1)
        ps_ss = ctx.enter_context(nc.psum_tensor("ps_ss", [P, 2, 512], F32))
        ps_s = (ps_ss[:, 0, :], ps_ss[:, 1, :])
        ps_s0, ps_s1 = ps_s

        cst = sb("cst", [P, C_END])
        ident = cst[:, C_ID:C_ID + P]
        wg_i = sb("wg_i", [P, HC, D], I32)
        wu_i = sb("wu_i", [P, HC, D], I32)
        wd_i = sb("wd_i", [P, HC, P], I32)
        wg_f = sb("wg_f", [P, HC, D])
        wu_f = sb("wu_f", [P, HC, D])
        wd_f = sb("wd_f", [P, HC, P])
        wgT = sb("wgT", [P, HC, P])
        wuT = sb("wuT", [P, HC, P])
        wdT = sb("wdT", [P, HC, D])
        wckr = sb("wckr", [P, KD])
        wiq = sb("wiq", [P, NI * DH])
        wik = sb("wik", [P, 2 * DH])
        iw_b = sb("iw_b", [P, NI])
        wuq_s = sb("wuq_s", [DQ, NH * DH])
        wuk_s = sb("wuk_s", [DC, NH * DH])
        wuv_s = sb("wuv_s", [DC, NH * DH])
        wdq_s = sb("wdq_s", [P, DQ])
        wout_s = sb("wout_s", [P, NH // 2, D])
        up_T = sb("up_T", [P, NH // 2, DQ + 2 * DC])
        wdqT = sb("wdqT", [DQ, P])
        wq64 = sb("wq64", [DQ, NH, KD])
        wqf = sb("wqf", [P, NH * KD])
        wvo = sb("wvo", [P, 2, D])
        delta = sb("delta", [P, 8, HALF])
        trig = sb("trig", [P, NTRIG, 4, HALF])
        trt = sb("trt", [P, 2, NTRIG, HALF])

        xs = sb("xs", [P, TILES, D])
        stats = {k: sb("stats" + k, [P, 6]) for k in "1m2"}
        mv = {k: sb("mv" + k, [P, 2]) for k in "1m2"}
        rstd = {k: sb("rstd" + k, [P, 1]) for k in "1m2"}
        rln = {k: sb("rln" + k, [P, 1]) for k in "1m2"}
        eps = sb("eps", [P, 1])
        xn = {k: sb("xn" + k, [P, D]) for k in "1m2"}
        xnT = {k: sb("xnT" + k, [P, P]) for k in "1m2"}
        x1nT = xnT["m"]
        f_abs = sb("f_abs", [P, HID])
        f_ln = sb("f_ln", [P, HID])
        f_sig = sb("f_sig", [P, HID])
        f_gu = sb("f_gu", [P, HID])
        hid = sb("hid", [P, HC, P])

        qiT = sb("qiT", [P, NI // 2, P])
        kiT = sb("kiT", [P, BATCH, LEN])
        pos_s = sb("pos_s", [P, NI, ICOLS])
        isc = sb("isc", [P, ICOLS])
        top8 = sb("top8", [P, SEL])
        idx = sb("idx", [P, SEL], U32)
        idxT = sb("idxT", [P, RING, NG], U32)

        k_abs = sb("k_abs", [P, DR])
        k_ln = sb("k_ln", [P, DR])
        rows = sb("rows", [P, RING, KD + DR])
        k_rot = sb("k_rot", [P, 2 * DR])
        krow = sb("krow", [P, 2, KD])
        keysT = sb("keysT", [P, RING, LW + P])
        c_win = sb("c_win", [WIN, RING, P // QUAD, DC])
        gath = sb("gath", [P, RING, NG, KD])
        g_rot = sb("g_rot", [P, 2 * GROUP, 2 * DR])

        q_abs = sb("q_abs", [P, NH, DR])
        q_ln = sb("q_ln", [P, NH, DR])
        q_mu = sb("q_mu", [P, NH, 2 * DR])
        q_rot = sb("q_rot", [P, NH, 2 * DR])
        qrow = sb("qrow", [P, 2, NH, KD])
        qT = sb("qT", [P, RING, 2, ND, QUAD, NH])

        kT = sb("kT", [P, 2, 512])
        sm = sb("sm", [P, 2, SW])
        mx = sb("mx", [P, 2])
        nmx = sb("nmx", [P, 2])
        den = sb("den", [P, 2])
        rden = sb("rden", [P, 2])
        pr = sb("pr", [P, 2, 2, SW])
        prT = sb("prT", [P, 2, 2, SC // NH, NH])
        prTw = sb("prTw", [WIN, 2, 2, QUAD, NH])
        oT = sb("oT", [P, 2, P, 2])

        x_in = [sem("x_first_in"), sem("x_rest_in")]
        ffn_w_in = [sem("w_gate_in"), sem("w_up_in"), sem("w_down_in")]
        cst_in, proj_w_in, lat_w_in, out_done = sem("cst_in"), sem("proj_w_in"), sem("lat_w_in"), sem("out_done")
        table_in = [sem(f"table_in{r}") for r in range(RING)]
        gathered = [[sem(f"gathered{r}_{d}") for d in range(ND)] for r in range(RING)]
        R = {m: sem(m) for m in (
            "wf", "eps", "rl1", "rlm", "rl2", "w_T", "w_Ts", "trig_e", "trig_s", "trig_a", "trig_sin", "trig_done",
            "lat_T", "lat_Ts", "lat_w", "lat_ws", "wqf_p", "wqf_s",
            "x1_down", "x1", "x2_y", "x2", "x3_down", "x3",
            "st1", "mv1", "rs1", "xn1", "xT1", "xTs1", "stm", "mvm", "rsm", "xnm", "xTm", "xTsm",
            "st2", "mv2", "rs2", "xn2", "xT2", "xTs2",
            "gu1", "ab1", "ex1", "ln1", "lsig1", "sig1", "gu_s1", "hid1",
            "gu2", "ab2", "ex2", "ln2", "lsig2", "sig2", "gu_s2", "hid2",
            "proj", "qki", "k_ab", "k_ex", "k_lnd", "rows_c", "rows_mu", "rows_all", "krot_m", "krow_done",
            "iscore", "irelu", "isum", "top", "topi", "idx_T", "idx_done",
            "qproj", "q_ab", "q_ex", "q_lnd", "q_c", "q_mud", "q_rm", "qrow_done", "qT_p", "qT_done",
            "keysT_p", "keysT_done", "cwin_p", "cwin_done",
            "g_rm", "g_done", "kT_p", "kT_done", "score", "smax", "nmax", "prob", "rdend", "prob_n",
            "prT_p", "prT_done", "value", "o_done")}

        block = ctx.enter_context(nc.Block())

        @block.sync
        def _(sp):
            sp.dma_start(xs[:, 0, :], x[0, 0:P, :]).then_inc(x_in[0], 16)
            sp.dma_start(wg_i[:, :, :], w_gate.rearrange("(c p) d -> p c d", p=P)).then_inc(ffn_w_in[0], 16)
            sp.dma_start(wd_i[:, :, :], w_down.rearrange("d (c p) -> d c p", p=P)).then_inc(ffn_w_in[2], 16)
            for src, dst in ((w_dkv, wckr[:, 0:DC]), (w_kr, wckr[:, DC:KD]), (iwq, wiq[:, :]),
                             (iwk, wik[:, 0:DH]), (iwk, wik[:, DH:2 * DH])):
                sp.dma_start(dst, src).then_inc(proj_w_in, 16)
            for b in range(BATCH):
                lo = 1 if b == 0 else 0
                sp.dma_start(xs[:, b * TPB + lo:(b + 1) * TPB, :],
                             x[b, lo * P:, :].rearrange("(t p) d -> p t d", p=P)).then_inc(x_in[1], 16)

            def table_rows(n):
                sp.wait_ge(R["rows_all"], 2 * (n + 1))
                sp.wait_ge(R["rows_mu"], n + 1)
                sp.wait_ge(R["rows_c"], 2 * n + 1)
                sp.dma_start(table[n * P:(n + 1) * P, :], rows[:, n % RING, 0:KD]).then_inc(table_in[n % RING], 16)

            def store(n):
                sp.wait_ge(R["x3"], n + 1)
                b, i = n // TPB, n % TPB
                sp.dma_start(out[b, i * P:(i + 1) * P, :], xs[:, n, :]).then_inc(out_done, 16)

            run_steps({"krow": table_rows, "store": store})
            sp.wait_ge(out_done, 16 * TILES)

        @block.gpsimd
        def _(pool):
            for n in range(TILES):
                pool.wait_ge(R["idx_done"], n + 1)
                pool.wait_ge(table_in[n % RING], 16 * (n // RING + 1))
                for g in range(NG):
                    pool.indirect_dma_start(
                        gath[:, n % RING, slot(g), :], None, table[0:(n + 1) * P, :],
                        bass.IndirectOffsetOnAxis(ap=idxT[:, n % RING, g:g + 1], axis=0),
                    ).then_inc(gathered[n % RING][g // (2 * GROUP)], 16)

        @block.scalar
        def _(act):
            act.dma_start(cst[:, :], consts).then_inc(cst_in, 16)
            act.dma_start(wu_i[:, :, :], w_up.rearrange("(c p) d -> p c d", p=P)).then_inc(ffn_w_in[1], 16)
            act.dma_start(delta[:, 0, :], raw_delta.rearrange("(a d) -> a d", a=1).partition_broadcast(P)).then_inc(cst_in, 16)
            act.dma_start(iw_b[:, :], iw.rearrange("(a d) -> a d", a=1).partition_broadcast(P)).then_inc(cst_in, 16)
            for src, dst in ((w_uq, wuq_s[:, :]), (w_uk, wuk_s[:, :]), (w_uv, wuv_s[:, :]), (w_dq, wdq_s[:, :]),
                             (w_out.rearrange("(c p) d -> p c d", p=P), wout_s[:, :, :]),
                             (w_qr.rearrange("q (h r) -> q h r", r=DR), wq64[:, :, DC:KD])):
                act.dma_start(dst, src).then_inc(lat_w_in, 16)

            act.wait_ge(cst_in, 48)
            nc.scalar.activation(delta[:, 1, :], delta[:, 0, :], ACT.Exp, scale=-1.0).then_inc(R["trig_e"], 1)
            act.wait_ge(R["eps"], 1)
            act.wait_ge(R["trig_a"], 1)
            nc.scalar.activation(delta[:, 5:7, :], delta[:, 3:5, :], ACT.Sin).then_inc(R["trig_sin"], 1)
            nc.scalar.preload_act_table_set("natural_log_exp_and_others")
            act.wait_ge(R["w_T"], 3)
            nc.scalar.copy(wgT[:, :, :].rearrange("p a b -> p (a b)"), ps_f1[:, 0:HID])
            nc.scalar.copy(wuT[:, :, :].rearrange("p a b -> p (a b)"), ps_f2[:, 0:HID])
            nc.scalar.copy(wdT[:, :, :].rearrange("p a b -> p (a b)"), ps_i0[:, 0:HID]).then_inc(R["w_Ts"], 1)

            def setup():
                act.wait_ge(R["lat_T"], 1)
                nc.scalar.copy(up_T[:, :, :].rearrange("p a b -> p (a b)"), ps_s0[:, :])
                nc.scalar.copy(wdqT[:, :], ps_s1[0:DQ, 0:P]).then_inc(R["lat_Ts"], 1)
                act.wait_ge(R["lat_w"], 1)
                act.wait_ge(lat_w_in, 96)
                for e in range(2):
                    q4 = (ps_tk, ps_tp)[e][0:DQ, 0:4 * DC].rearrange("p (h c) -> p h c", c=DC)
                    nc.scalar.copy(wq64[:, e::2, 0:DC], q4).then_inc(R["lat_ws"], 1)
                for e in range(2):
                    nc.scalar.copy(wvo[:, e, :], ps_s[e][:, 0:D]).then_inc(R["lat_ws"], 1)
                act.wait_ge(R["wqf_p"], 1)
                nc.scalar.copy(wqf[:, :], ps_tk[:, :]).then_inc(R["wqf_s"], 1)

            def stat(k, n):
                act.wait_ge(R["mv" + k], n + 1)
                nc.scalar.activation(rln[k][:, :], mv[k][:, 1:2], ACT.Ln, bias=eps[:, 0:1]).then_inc(R["rl" + k], 1)
                act.wait_ge(R["rl" + k], n + 1)
                nc.scalar.activation(rstd[k][:, :], rln[k][:, :], ACT.Exp, scale=-0.5).then_inc(R["rs" + k], 1)

            def turned(k):
                def part(n):
                    act.wait_ge(R["xT" + k], n + 1)
                    nc.scalar.copy(xnT[k][:, :], ps_f1[:, HID:512]).then_inc(R["xTs" + k], 1)
                return part

            def gate(k):
                def part(n):
                    act.wait_ge(R["gu" + k], n + 1)
                    nc.scalar.activation(f_abs[:, :], ps_f1[:, 0:HID], ACT.Abs).then_inc(R["ab" + k], 1)
                    act.wait_ge(R["ab" + k], n + 1)
                    nc.scalar.activation(f_abs[:, :], f_abs[:, :], ACT.Exp, scale=-1.0).then_inc(R["ex" + k], 1)
                    act.wait_ge(R["ex" + k], n + 1)
                    nc.scalar.activation(f_ln[:, :], f_abs[:, :], ACT.Ln, bias=1.0).then_inc(R["ln" + k], 1)
                return part

            def sigmoid(k):
                def part(n):
                    act.wait_ge(R["lsig" + k], n + 1)
                    nc.scalar.activation(f_sig[:, :], f_sig[:, :], ACT.Exp).then_inc(R["sig" + k], 1)
                return part

            def proj(n):
                b, i, r = n // TPB, n % TPB, n % RING
                act.wait_ge(R["proj"], n + 1)
                for c in range(NI // 2):
                    nc.scalar.copy(qiT[:, c, :].rearrange("p (j g) -> p g j", j=GROUP),
                                   ps_i1[:, c * P:(c + 1) * P].rearrange("p (g j) -> p g j", j=GROUP))
                nc.scalar.copy(kiT[:, b, i * P:(i + 1) * P], ps_i1[:, 2 * P:3 * P]).then_inc(R["qki"], 1)
                nc.scalar.activation(k_abs[:, :], ps_f2[:, DC:KD], ACT.Abs).then_inc(R["k_ab"], 1)
                nc.scalar.copy(rows[:, r, 0:DC], ps_f2[:, 0:DC]).then_inc(R["rows_c"], 1)
                act.wait_ge(R["k_ab"], n + 1)
                nc.scalar.activation(k_abs[:, :], k_abs[:, :], ACT.Exp, scale=-1.0).then_inc(R["k_ex"], 1)
                act.wait_ge(R["k_ex"], n + 1)
                nc.scalar.activation(k_ln[:, :], k_abs[:, :], ACT.Ln, bias=1.0).then_inc(R["k_lnd"], 1)

            def index(n):
                f = fills_before(n)
                for a, w in chunks(n):
                    for h in range(NI):
                        f += 1
                        act.wait_ge(R["iscore"], f)
                        nc.scalar.activation(pos_s[:, h, a:a + w], ps_i[h % 2][:, 0:w], ACT.Relu).then_inc(R["irelu"], 1)

            def krow_c(n):
                src = rows[:, n % RING, 0:DC]
                act.wait_ge(R["rows_c"], 2 * n + 1)
                nc.scalar.copy(krow[:, 0, 0:DC], src)
                nc.scalar.copy(krow[:, 1, 0:DC], src).then_inc(R["rows_c"], 1)

            def query(n):
                act.wait_ge(R["qproj"], n + 1)
                q = ps_i0[:, :].rearrange("p (h k) -> p h k", k=KD)
                nc.scalar.activation(q_abs[:, :, :], q[:, :, DC:KD], ACT.Abs).then_inc(R["q_ab"], 1)
                nc.scalar.copy(qrow[:, 0, :, 0:DC], q[:, :, 0:DC])
                act.wait_ge(R["q_ab"], n + 1)
                nc.scalar.activation(q_abs[:, :, :], q_abs[:, :, :], ACT.Exp, scale=-1.0).then_inc(R["q_ex"], 1)
                nc.scalar.copy(qrow[:, 1, :, 0:DC], q[:, :, 0:DC]).then_inc(R["q_c"], 1)
                act.wait_ge(R["q_ex"], n + 1)
                nc.scalar.activation(q_ln[:, :, :], q_abs[:, :, :], ACT.Ln, bias=1.0).then_inc(R["q_lnd"], 1)

            def keys_turned(n):
                act.wait_ge(R["keysT_p"], n + 1)
                if n % TPB < TPB - 1:
                    nc.scalar.copy(keysT[:, (n + 1) % RING, 0:LW], ps_i1[:, P - LW:P])
                nc.scalar.copy(keysT[:, n % RING, LW:LW + P], ps_i1[:, 0:P]).then_inc(R["keysT_done"], 1)

            def queryT(n):
                r = n % RING
                for v in range(2):
                    act.wait_ge(R["qT_p"], 2 * n + v + 1)
                    for e in range(2):
                        src = ps_i[v][e * KD:(e + 1) * KD, :].rearrange("k (h d q t) -> k q d h t", h=NH // 2, q=2, t=QUAD)
                        for par in range(2):
                            for d in range(ND):
                                dst = qT[par * KD:(par + 1) * KD, r, v, d, :, e::2].rearrange("k t h -> k h t")
                                last = nc.scalar.copy(dst, src[:, par, d])
                    last.then_inc(R["qT_done"], 1)

            def cwin(n):
                act.wait_ge(R["cwin_p"], n + 1)
                nc.scalar.copy(c_win[:, n % RING, :, :].rearrange("p q c -> p (q c)"),
                               ps_i1[0:WIN, P:P + (P // QUAD) * DC]).then_inc(R["cwin_done"], 1)

            def key(n, d):
                k = n * ND + d
                act.wait_ge(R["kT_p"], k + 1)
                nc.scalar.copy(kT[:, k % 2, :], ps_tk[:, :]).then_inc(R["kT_done"], 1)

            def score(n, d):
                k = n * ND + d
                act.wait_ge(R["nmax"], k + 1)
                for q in range(2):
                    last = nc.scalar.activation(pr[:, k % 2, q, :], sm[:, q, :], ACT.Exp, bias=nmx[:, q:q + 1],
                                                scale=SCALE, accum_out=den[:, q:q + 1])
                last.then_inc(R["prob"], 1)

            def turn(n, d):
                k = n * ND + d
                act.wait_ge(R["prT_p"], k + 1)
                nc.scalar.copy(prT[:, k % 2].rearrange("p q t h -> p (q t h)"), ps_tp[:, 0:2 * SC])
                nc.scalar.copy(prTw[:, k % 2].rearrange("p q t h -> p (q t h)"),
                               ps_tp[0:WIN, 2 * SC:512]).then_inc(R["prT_done"], 1)

            run_steps({"stat1": lambda n: stat("1", n), "norm1": turned("1"), "gate1": gate("1"), "act1": sigmoid("1"),
                       "hid1": lambda n: stat("m", n), "normm": turned("m"), "proj": proj, "index": index,
                       "krow": krow_c, "query": query, "keysT": keys_turned, "cwin": cwin, "queryT": queryT,
                       "key": key, "score": score, "turn": turn, "mix": lambda n: stat("2", n),
                       "norm2": turned("2"), "gate2": gate("2"), "act2": sigmoid("2")}, setup)

        @block.vector
        def _(dve):
            nc.vector.memset(eps[:, :], EPS).then_inc(R["eps"], 1)
            for k, (src, dst) in enumerate(((wg_i, wg_f), (wu_i, wu_f), (wd_i, wd_f))):
                dve.wait_ge(ffn_w_in[k], 16)
                nc.vector.tensor_scalar(dst[:, :, :], src[:, :, :], WSCALE, None, ALU.mult).then_inc(R["wf"], 1)
            pi = float(np.pi)
            top = 3.1415925
            dve.wait_ge(R["trig_e"], 1)
            nc.vector.tensor_scalar(delta[:, 2, :], delta[:, 1, :], 1.0, None, ALU.add).then_inc(R["trig_s"], 1)
            dve.wait_ge(R["trig_s"], 1)
            nc.vector.reciprocal(delta[:, 2, :], delta[:, 2, :]).then_inc(R["trig_s"], 1)
            dve.wait_ge(R["trig_s"], 2)
            nc.vector.tensor_scalar(delta[:, 3, :], delta[:, 2, :], pi, None, ALU.mult)
            nc.vector.tensor_scalar(delta[:, 4, :], delta[:, 2, :], -2.0 * pi, pi, ALU.mult, ALU.add).then_inc(R["trig_s"], 1)
            dve.wait_ge(R["trig_s"], 3)
            nc.vector.tensor_scalar(delta[:, 3:5, :], delta[:, 3:5, :], top, -top, ALU.min, ALU.max).then_inc(R["trig_a"], 1)

            def trig_tables():
                done = 0
                cd, sd = delta[:, 7:8, :], delta[:, 6:7, :]
                dve.wait_ge(R["trig_sin"], 1)
                nc.vector.tensor_tensor(delta[:, 7, :], delta[:, 5, :], delta[:, 5, :], ALU.mult).then_inc(R["trig_s"], 1)
                dve.wait_ge(R["trig_s"], 4)
                nc.vector.tensor_scalar(delta[:, 7, :], delta[:, 7, :], -2.0, 1.0, ALU.mult, ALU.add).then_inc(R["trig_s"], 1)
                dve.wait_ge(R["trig_s"], 5)
                dve.wait_ge(cst_in, 48)
                cb = cst[:, C_COS:C_SIN].rearrange("p (n f) -> p n f", f=HALF)
                sn = cst[:, C_SIN:C_END].rearrange("p (n f) -> p n f", f=HALF)
                full = [P, NTRIG, HALF]
                for j, (u, v, op) in enumerate(((cb, sn, ALU.add), (sn, cb, ALU.subtract))):
                    nc.vector.tensor_tensor(trt[:, 0, :, :], u, cd.to_broadcast(full), ALU.mult)
                    nc.vector.tensor_tensor(trt[:, 1, :, :], v, sd.to_broadcast(full), ALU.mult).then_inc(R["trig_s"], 1)
                    dve.wait_ge(R["trig_s"], 6 + 2 * j)
                    dst = trig[:, :, 0, :] if j == 0 else trig[:, :, 3, :]
                    nc.vector.tensor_tensor(dst, trt[:, 0, :, :], trt[:, 1, :, :], op).then_inc(R["trig_s"], 1)
                    dve.wait_ge(R["trig_s"], 7 + 2 * j)
                nc.vector.tensor_copy(trig[:, :, 1, :], trig[:, :, 0, :])
                nc.vector.tensor_scalar(trig[:, :, 2, :], trig[:, :, 3, :], -1.0, None, ALU.mult).then_inc(R["trig_done"], 1)
                dve.wait_ge(R["trig_done"], 1)

            def stat(k, n):
                nc.vector.bn_stats(stats[k][:, :], xs[:, n, :]).then_inc(R["st" + k], 1)
                dve.wait_ge(R["st" + k], n + 1)
                nc.vector.bn_aggr(mv[k][:, :], stats[k][:, :]).then_inc(R["mv" + k], 1)

            def normed(k):
                def part(n):
                    dve.wait_ge(R["rs" + k], n + 1)
                    nc.vector.tensor_scalar(xn[k][:, :], xs[:, n, :], mv[k][:, 0:1], rstd[k][:, 0:1], ALU.subtract,
                                            ALU.mult).then_inc(R["xn" + k], 1)
                return part

            def stat1(n):
                dve.wait_ge(x_in[min(n, 1)], 16 if n == 0 else 32)
                stat("1", n)

            def log_sigmoid(k):
                def part(n):
                    dve.wait_ge(R["ln" + k], n + 1)
                    nc.vector.scalar_tensor_tensor(f_sig[:, :], ps_f1[:, 0:HID], 0.0, f_ln[:, :],
                                                   ALU.min, ALU.subtract).then_inc(R["lsig" + k], 1)
                return part

            def hidden(k):
                def part(n):
                    dve.wait_ge(R["sig" + k], n + 1)
                    nc.vector.tensor_tensor(f_gu[:, :], ps_f1[:, 0:HID], f_sig[:, :], ALU.mult).then_inc(R["gu_s" + k], 1)
                    dve.wait_ge(R["gu_s" + k], n + 1)
                    nc.vector.tensor_tensor(hid[:, :, :].rearrange("p a b -> p (a b)"), ps_f2[:, 0:HID], f_gu[:, :],
                                            ALU.mult).then_inc(R["hid" + k], 1)
                return part

            def hid1(n):
                hidden("1")(n)
                dve.wait_ge(R["x1_down"], n + 1)
                nc.vector.scalar_tensor_tensor(xs[:, n, :], ps_f2[:, HID:512], 0.5, xs[:, n, :],
                                               ALU.mult, ALU.add).then_inc(R["x1"], 1)
                dve.wait_ge(R["x1"], n + 1)
                stat("m", n)
                if n == 0:
                    trig_tables()

            def krow_rot(n):
                i, r = n % TPB, n % RING
                dve.wait_ge(R["k_lnd"], n + 1)
                for dst, a in ((DC, 0), (DC + DR, HALF), (DC + DR + HALF, 0)):
                    w = DR if dst == DC else HALF
                    ins = nc.vector.scalar_tensor_tensor(rows[:, r, dst:dst + w], ps_f2[:, DC + a:DC + a + w], 0.0,
                                                         k_ln[:, a:a + w], ALU.max, ALU.add)
                    ins.then_inc(R["rows_mu"] if dst == DC else R["rows_all"], 1)
                dve.wait_ge(R["rows_all"], 2 * (n + 1))
                dve.wait_ge(R["rows_mu"], n + 1)
                nc.vector.tensor_tensor(k_rot[:, :], rows[:, r, DC:KD + DR], trig[:, i, :, :].rearrange("p a f -> p (a f)"),
                                        ALU.mult).then_inc(R["krot_m"], 1)
                dve.wait_ge(R["krot_m"], n + 1)
                for c in range(2):
                    nc.vector.tensor_tensor(krow[:, c, DC:KD], k_rot[:, 0:DR], k_rot[:, DR:2 * DR],
                                            ALU.add).then_inc(R["krow_done"], 1)

            def index(n):
                i = n % TPB
                f = fills_before(n)
                s = isum_before(n)
                for a, w in chunks(n):
                    for h in range(NI):
                        f += 1
                        dve.wait_ge(R["irelu"], f)
                        dst = isc[:, a:a + w]
                        if h == 0:
                            ins = nc.vector.tensor_scalar(dst, pos_s[:, 0, a:a + w], iw_b[:, 0:1], None, ALU.mult)
                        else:
                            dve.wait_ge(R["isum"], s)
                            ins = nc.vector.scalar_tensor_tensor(dst, pos_s[:, h, a:a + w], iw_b[:, h:h + 1], dst,
                                                                 ALU.mult, ALU.add)
                        ins.then_inc(R["isum"], 1)
                        s += 1
                m = cst[:, C_M0:C_M0 + TOPK] if i == 0 else cst[:, C_M1:C_M1 + P]
                w = columns(n)
                dst = isc[:, w - m.shape[1]:w]
                dve.wait_ge(R["isum"], s)
                nc.vector.tensor_tensor(dst, dst, m, ALU.add).then_inc(R["isum"], 1)
                dve.wait_ge(R["isum"], s + 1)

            def isum_before(n):
                return sum(NI * len(chunks(m)) + 1 for m in range(n))

            def pick(k):
                return lambda n: pick_eight(n, k)

            def pick_eight(n, k):
                w, e = columns(n), slice(8 * k, 8 * k + 8)
                base = 7 * n + 2 * k
                nc.vector.max(top8[:, e], isc[:, 0:w]).then_inc(R["top"], 1)
                dve.wait_ge(R["top"], base + 1)
                nc.vector.max_index(idx[:, e], top8[:, e], isc[:, 0:w]).then_inc(R["topi"], 1)
                if k < 3:
                    nc.vector.match_replace(isc[:, 0:w], top8[:, e], isc[:, 0:w], TAKEN).then_inc(R["top"], 1)
                    dve.wait_ge(R["top"], base + 2)
                else:
                    dve.wait_ge(R["topi"], 4 * n + 4)
                    r = n % RING
                    if n < TPB:
                        nc.vector.transpose(idxT[:, r, :], idx[:, :]).then_inc(R["idx_done"], 1)
                    else:
                        nc.vector.transpose(idxT[:, r, :], idx[:, :]).then_inc(R["idx_T"], 1)
                        dve.wait_ge(R["idx_T"], n - TPB + 1)
                        nc.vector.tensor_scalar(idxT[:, r, :], idxT[:, r, :], float(LEN), None, ALU.add).then_inc(R["idx_done"], 1)

            def query(n):
                i = n % TPB
                q = ps_i0[:, :].rearrange("p (h k) -> p h k", k=KD)
                dve.wait_ge(R["q_lnd"], n + 1)
                for dst, a in ((0, 0), (DR, HALF), (DR + HALF, 0)):
                    w = DR if dst == 0 else HALF
                    nc.vector.scalar_tensor_tensor(q_mu[:, :, dst:dst + w], q[:, :, DC + a:DC + a + w], 0.0,
                                                   q_ln[:, :, a:a + w], ALU.max, ALU.add).then_inc(R["q_mud"], 1)
                dve.wait_ge(R["q_mud"], 3 * (n + 1))
                for v in range(2):
                    tr = trig[:, i + v * TPB, :, :].rearrange("p (o a) f -> p o (a f)", o=1).to_broadcast([P, NH, 2 * DR])
                    nc.vector.tensor_tensor(q_rot[:, :, :], q_mu[:, :, :], tr, ALU.mult).then_inc(R["q_rm"], 1)
                    dve.wait_ge(R["q_rm"], 2 * n + v + 1)
                    nc.vector.tensor_tensor(qrow[:, v, :, DC:KD], q_rot[:, :, 0:DR], q_rot[:, :, DR:2 * DR],
                                            ALU.add).then_inc(R["qrow_done"], 1)
                    if v == 0:
                        dve.wait_ge(R["qrow_done"], 2 * n + 1)

            def key(n, d):
                r, k = n % RING, n * ND + d
                dve.wait_ge(gathered[r][d], 16 * 2 * GROUP * (n // RING + 1))
                gs = slice(2 * GROUP * d, 2 * GROUP * (d + 1))
                tr = trig[:, RANKS, :, :].rearrange("p (o a) f -> p o (a f)", o=1).to_broadcast([P, 2 * GROUP, 2 * DR])
                mu = gath[:, r, gs, DC:KD]
                nc.vector.tensor_tensor(g_rot[:, :, 0:DR], mu, tr[:, :, 0:DR], ALU.mult)
                nc.vector.tensor_tensor(g_rot[:, :, DR:DR + HALF], mu[:, :, HALF:DR], tr[:, :, DR:DR + HALF], ALU.mult)
                nc.vector.tensor_tensor(g_rot[:, :, DR + HALF:2 * DR], mu[:, :, 0:HALF], tr[:, :, DR + HALF:2 * DR],
                                        ALU.mult).then_inc(R["g_rm"], 1)
                dve.wait_ge(R["g_rm"], k + 1)
                nc.vector.tensor_tensor(gath[:, r, gs, DC:KD], g_rot[:, :, 0:DR], g_rot[:, :, DR:2 * DR],
                                        ALU.add).then_inc(R["g_done"], 1)

            def score(n, d):
                k = n * ND + d
                dve.wait_ge(R["score"], k + 1)
                for q in range(2):
                    first = n % TPB == 0 and 2 * d + q < LW // QUAD
                    m = cst[:, C_MS0:C_MS0 + SW] if first else cst[:, C_MS:C_MS + SW]
                    last = nc.vector.tensor_tensor_reduce(sm[:, q, :], ps_s[q][:, 0:SW], m, 1.0, -3.0e38, ALU.add,
                                                          ALU.max, mx[:, q:q + 1])
                last.then_inc(R["smax"], 1)
                dve.wait_ge(R["smax"], k + 1)
                nc.vector.tensor_scalar(nmx[:, :], mx[:, :], -SCALE, None, ALU.mult).then_inc(R["nmax"], 1)

            def turn(n, d):
                k = n * ND + d
                dve.wait_ge(R["prob"], k + 1)
                nc.vector.reciprocal(rden[:, :], den[:, :]).then_inc(R["rdend"], 1)
                dve.wait_ge(R["rdend"], k + 1)
                for q in range(2):
                    last = nc.vector.tensor_scalar(pr[:, k % 2, q, :], pr[:, k % 2, q, :], rden[:, q:q + 1], None, ALU.mult)
                last.then_inc(R["prob_n"], 1)

            def value(n, d):
                k = n * ND + d
                dve.wait_ge(R["value"], k + 1)
                nc.vector.tensor_copy(oT[:, n % 2, d * DUO:(d + 1) * DUO, :].rearrange("c (q t) h -> c q (t h)", q=2),
                                      ps_ss[:, :, 256:256 + 2 * QUAD]).then_inc(R["o_done"], 1)

            def mix(n):
                dve.wait_ge(R["x2_y"], n + 1)
                nc.vector.tensor_tensor(xs[:, n, :], ps_f2[:, HID:512], xs[:, n, :], ALU.add).then_inc(R["x2"], 1)
                dve.wait_ge(R["x2"], n + 1)
                stat("2", n)

            def hid2(n):
                hidden("2")(n)
                dve.wait_ge(R["x3_down"], n + 1)
                nc.vector.scalar_tensor_tensor(xs[:, n, :], ps_f2[:, HID:512], 0.5, xs[:, n, :],
                                               ALU.mult, ALU.add).then_inc(R["x3"], 1)

            run_steps({"stat1": stat1, "norm1": normed("1"), "act1": log_sigmoid("1"), "hid1": hid1,
                       "normm": normed("m"), "krow": krow_rot, "index": index, "pick0": pick(0), "pick1": pick(1),
                       "pick2": pick(2), "pick3": pick(3), "rope": query, "key": key, "score": score, "turn": turn,
                       "value": value, "mix": mix, "norm2": normed("2"), "act2": log_sigmoid("2"), "hid2": hid2})

        @block.tensor
        def _(pe):
            pe.wait_ge(cst_in, 48)
            for k, (src, dst) in enumerate(((wg_f, ps_f1), (wu_f, ps_f2), (wd_f, ps_i0))):
                pe.wait_ge(R["wf"], k + 1)
                for c in range(HC):
                    last = nc.tensor.transpose(dst[:, c * P:(c + 1) * P], src[:, c, :], ident)
                last.then_inc(R["w_T"], 1)

            def setup():
                pe.wait_ge(lat_w_in, 96)
                for c in range(NH // 2):
                    cols = slice(c * P, (c + 1) * P)
                    nc.tensor.transpose(ps_s0[:, c * P:c * P + DQ], wuq_s[:, cols], ident[0:DQ, 0:DQ])
                    nc.tensor.transpose(ps_s0[:, c * P + DQ:c * P + DQ + DC], wuk_s[:, cols], ident[0:DC, 0:DC])
                    nc.tensor.transpose(ps_s0[:, c * P + DQ + DC:(c + 1) * P], wuv_s[:, cols], ident[0:DC, 0:DC])
                nc.tensor.transpose(ps_s1[0:DQ, 0:P], wdq_s[:, :], ident).then_inc(R["lat_T"], 1)
                pe.wait_ge(R["lat_Ts"], 1)
                for h in range(NH):
                    e, c = h % 2, h // 2
                    rows_h = slice(e * DH, (e + 1) * DH)
                    nc.tensor.matmul((ps_tk, ps_tp)[e][0:DQ, c * DC:(c + 1) * DC], up_T[rows_h, c, 0:DQ],
                                     up_T[rows_h, c, DQ:DQ + DC], start=True, stop=True)
                    last = nc.tensor.matmul(ps_s[e][c * DC:(c + 1) * DC, 0:D], up_T[rows_h, c, DQ + DC:DQ + 2 * DC],
                                            wout_s[rows_h, c, :], start=True, stop=True)
                last.then_inc(R["lat_w"], 1)
                pe.wait_ge(R["lat_ws"], 4)
                nc.tensor.matmul(ps_tk[:, :], wdqT[:, :], wq64[:, :, :].rearrange("p h k -> p (h k)"),
                                 start=True, stop=True).then_inc(R["wqf_p"], 1)
                pe.wait_ge(R["wqf_s"], 1)

            def turned(k):
                def part(n):
                    if n == 0 and k == "1":
                        pe.wait_ge(R["w_Ts"], 1)
                    if k == "m" and n >= AHEAD - BEHIND + 1:
                        pe.wait_ge(R["gu_s2"], n - (AHEAD - BEHIND))
                    if k == "1" and n:
                        pe.wait_ge(R["xTsm"], n)
                    pe.wait_ge(R["xn" + k], n + 1)
                    nc.tensor.transpose(ps_f1[:, HID:512], xn[k][:, :], ident).then_inc(R["xT" + k], 1)
                return part

            def gate_up(k, n):
                if k == "1" and n:
                    pe.wait_ge(R["rows_all"], 2 * n)
                pe.wait_ge(R["xTs" + k], n + 1)
                for w, dst in ((wgT, ps_f1), (wuT, ps_f2)):
                    for c in range(HC):
                        last = nc.tensor.matmul(dst[:, c * P:(c + 1) * P], w[:, c, :], xnT[k][:, :], start=True, stop=True)
                last.then_inc(R["gu" + k], 1)

            def down(k, n):
                pe.wait_ge(R["hid" + k], n + 1)
                for c in range(HC):
                    last = nc.tensor.matmul(ps_f2[:, HID:512], hid[:, c, :], wdT[:, c, :], start=(c == 0), stop=(c == HC - 1))
                last.then_inc(R["x1_down" if k == "1" else "x3_down"], 1)

            def proj(n):
                if n == 0:
                    pe.wait_ge(proj_w_in, 80)
                pe.wait_ge(R["xTsm"], n + 1)
                if n:
                    pe.wait_ge(R["qT_done"], 2 * n)
                if n >= AHEAD - BEHIND + 1:
                    pe.wait_ge(R["x3"], n - (AHEAD - BEHIND))
                for c in range(NI // 2):
                    nc.tensor.matmul(ps_i1[:, c * P:(c + 1) * P], wiq[:, c * P:(c + 1) * P], x1nT[:, :], start=True, stop=True)
                nc.tensor.matmul(ps_i1[:, 2 * P:3 * P], wik[:, :], x1nT[:, :], start=True, stop=True)
                nc.tensor.matmul(ps_f2[:, 0:KD], x1nT[:, :], wckr[:, :], start=True, stop=True).then_inc(R["proj"], 1)

            def index(n):
                b = n // TPB
                pe.wait_ge(R["qki"], n + 1)
                f = fills_before(n)
                for c, (a, w) in enumerate(chunks(n)):
                    for h in range(NI):
                        e = h % 2
                        if c or h >= 2:
                            pe.wait_ge(R["irelu"], f - 1)
                        q = qiT[e * DH:(e + 1) * DH, h // 2, :]
                        nc.tensor.matmul(ps_i[e][:, 0:w], q, kiT[e * DH:(e + 1) * DH, b, a:a + w],
                                         start=True, stop=True).then_inc(R["iscore"], 1)
                        f += 1

            def query(n):
                pe.wait_ge(R["irelu"], fills_before(n + 1))
                nc.tensor.matmul(ps_i0[:, :], x1nT[:, :], wqf[:, :], start=True, stop=True).then_inc(R["qproj"], 1)

            def keys_turned(n):
                pe.wait_ge(R["krow_done"], 2 * (n + 1))
                pe.wait_ge(R["rows_c"], 2 * (n + 1))
                nc.tensor.transpose(ps_i1[:, 0:P], krow[:, :, :].rearrange("p a b -> p (a b)"), ident).then_inc(R["keysT_p"], 1)

            def queryT(n):
                pe.wait_ge(R["q_c"], n + 1)
                pe.wait_ge(R["cwin_done"], n + 1)
                for v in range(2):
                    pe.wait_ge(R["qrow_done"], 2 * n + v + 1)
                    for c in range(NH // 2):
                        last = nc.tensor.transpose(ps_i[v][:, c * P:(c + 1) * P],
                                                   qrow[:, v, 2 * c:2 * c + 2, :].rearrange("p a b -> p (a b)"), ident)
                    last.then_inc(R["qT_p"], 1)

            def cwin(n):
                r = n % RING
                pe.wait_ge(R["keysT_done"], n + 1)
                for q in range(P // QUAD):
                    a = window(n, q)
                    last = nc.tensor.transpose(ps_i1[0:WIN, P + q * DC:P + (q + 1) * DC], keysT[0:DC, r, a:a + WIN], ident[0:DC, 0:DC])
                last.then_inc(R["cwin_p"], 1)

            def window(n, q):
                return max(QUAD * q, LW) if n % TPB == 0 else QUAD * q

            def key(n, d):
                r, k = n % RING, n * ND + d
                pe.wait_ge(R["g_done"], k + 1)
                if k:
                    pe.wait_ge(R["kT_done"], k)
                for g in range(GROUP):
                    a = slot(2 * GROUP * d + g)
                    pair = gath[:, r, a:a + 2, :].rearrange("p a k -> p (a k)")
                    last = nc.tensor.transpose(ps_tk[:, g * P:(g + 1) * P], pair, ident)
                last.then_inc(R["kT_p"], 1)

            def score(n, d):
                r, k = n % RING, n * ND + d
                pe.wait_ge(R["kT_done"], k + 1)
                pe.wait_ge(R["qT_done"], 2 * (n + 1))
                if k > 1:
                    pe.wait_ge(R["o_done"], k - 1)
                if k:
                    pe.wait_ge(R["smax"], k)
                for q in range(2):
                    half = slice(q * KD, (q + 1) * KD)
                    a = window(n, 2 * d + q)
                    nc.tensor.matmul(ps_s[q][:, SC:SW], qT[half, r, 1, d, :, :].rearrange("k t h -> k (t h)"),
                                     keysT[half, r, a:a + WIN], start=True, stop=True)
                    for g in range(GROUP):
                        last = nc.tensor.matmul(
                            ps_s[q][g * SEL:(g + 1) * SEL, 0:SC],
                            qT[half, r, 0, d, g * GROUP:(g + 1) * GROUP, :].rearrange("k t h -> k (t h)"),
                            kT[half, k % 2, g * P:(g + 1) * P], start=True, stop=True)
                last.then_inc(R["score"], 1)

            def turn(n, d):
                k = n * ND + d
                pe.wait_ge(R["prob_n"], k + 1)
                if k:
                    pe.wait_ge(R["prT_done"], k)
                for q in range(2):
                    nc.tensor.transpose(ps_tp[:, q * P:(q + 1) * P], pr[:, k % 2, q, 0:SC], ident)
                    last = nc.tensor.transpose(ps_tp[0:WIN, (2 + q) * P:(3 + q) * P], pr[:, k % 2, q, SC:SW], ident)
                last.then_inc(R["prT_p"], 1)

            def value(n, d):
                r, k = n % RING, n * ND + d
                pe.wait_ge(R["prT_done"], k + 1)
                pe.wait_ge(R["cwin_done"], n + 1)
                pe.wait_ge(R["smax"], min(k + 2, ND * TILES))
                for q in range(2):
                    for j in range(NH // 2):
                        nc.tensor.matmul(ps_s[q][j * DC:(j + 1) * DC, 256:256 + 2 * QUAD], c_win[:, r, 2 * d + q, :],
                                         prTw[:, k % 2, q, :, 2 * j:2 * j + 2],
                                         start=True, stop=False, skip_group_check=True)
                    for g in range(GROUP):
                        o = 256 + 2 * GROUP * g
                        for j in range(NH // 2):
                            last = nc.tensor.matmul(
                                ps_s[q][j * DC:(j + 1) * DC, o:o + 2 * GROUP],
                                gath[:, r, slot(2 * GROUP * d + GROUP * q + g), 0:DC],
                                prT[:, k % 2, q, g * GROUP:(g + 1) * GROUP, 2 * j:2 * j + 2],
                                start=False, stop=(g == GROUP - 1), skip_group_check=True)
                last.then_inc(R["value"], 1)

            def mix(n):
                pe.wait_ge(R["o_done"], ND * (n + 1))
                pe.wait_ge(R["x1"], min(n + AHEAD1 - BEHIND + 1, TILES))
                for e in range(2):
                    last = nc.tensor.matmul(ps_f2[:, HID:512], oT[:, n % 2, :, e], wvo[:, e, :], start=(e == 0), stop=(e == 1))
                last.then_inc(R["x2_y"], 1)

            run_steps({"norm1": turned("1"), "gate1": lambda n: gate_up("1", n), "hid1": lambda n: down("1", n),
                       "normm": turned("m"), "proj": proj, "index": index, "query": query, "keysT": keys_turned,
                       "cwin": cwin, "queryT": queryT, "key": key, "score": score, "turn": turn, "value": value,
                       "mix": mix, "norm2": turned("2"), "gate2": lambda n: gate_up("2", n),
                       "hid2": lambda n: down("2", n)}, setup)


_INS = ['L0_attn_x', 'L0_attn_W_dkv', 'L0_attn_W_uk', 'L0_attn_W_uv', 'L0_attn_W_dq', 'L0_attn_W_uq', 'L0_attn_W_qr',
        'L0_attn_W_kr', 'L0_attn_W_out', 'L0_attn_idx_wq', 'L0_attn_idx_wk', 'L0_attn_idx_w', 'L0_attn_raw_delta',
        'L0_ffn_w_gate', 'L0_ffn_w_up', 'L0_ffn_w_down']


def kernel(**inputs):
    import concourse.bacc as _bacc
    from concourse.bass_utils import run_bass_kernel_spmd as _run

    nc = _bacc.Bacc("TRN2", target_bir_lowering=False, num_devices=1)
    arrays, args = {}, []
    for name in _INS + ["shape_constants"]:
        a = shape_constants() if name == "shape_constants" else np.ascontiguousarray(inputs[name])
        arrays[f"in_{name}"] = a
        args.append(nc.dram_tensor(f"in_{name}", a.shape, mybir.dt.from_np(a.dtype), kind="ExternalInput").ap())
    out = nc.dram_tensor("out_0", (BATCH, LEN, D), F32, kind="ExternalOutput").ap()
    macaron_block(nc, *args, out)
    r = _run(nc, [arrays], core_ids=[0])
    return r.results[0]["out_0"]
```

```python
from contextlib import ExitStack

import numpy as np

import concourse.bass as bass
from concourse import mybir

ALU = mybir.AluOpType
ACT = mybir.ActivationFunctionType
F32 = mybir.dt.float32
I32 = mybir.dt.int32
U32 = mybir.dt.uint32

P = 128
BATCH, LEN = 2, 1024
D = 128
HID = 384
HC = HID // P
NH, DH = 8, 64
DC, DR, DQ = 32, 32, 64
HALF = DR // 2
NI = 4
TOPK, LW = 96, 64
SEL = TOPK - LW
KD = DC + DR

TPB = LEN // P
TILES = BATCH * TPB
RING = 4
WIN = 80
GROUP = P // SEL
QUAD = 16
NG = P // GROUP
DUO = 2 * QUAD
ND = P // DUO
SC = SEL * GROUP
SW = SC + WIN
ICOLS = LEN - LW
SCALE = float(KD + DR) ** -0.5
WSCALE = 1.0 / 127.0
NEG = -1.0e30
FUTURE = -1.0e38
TAKEN = -3.0e38
EPS = 1e-5
NTRIG = 2 * TPB + 1
RANKS = 2 * TPB

C_ID = 0
C_MS = C_ID + P
C_MS0 = C_MS + SW
C_M1 = C_MS0 + SW
C_M0 = C_M1 + P
C_COS = C_M0 + TOPK
C_SIN = C_COS + NTRIG * HALF
C_END = C_SIN + NTRIG * HALF


def shape_constants():
    c = np.zeros((P, C_END), np.float32)
    c[:, C_ID:C_ID + P] = np.eye(P)
    row = np.arange(P)
    t16 = row // NH
    col = np.arange(SC)
    diag = (t16[:, None] % GROUP) == (col[None, :] // SEL)
    w = np.arange(WIN)
    inside = (w[None, :] >= t16[:, None] + 1) & (w[None, :] <= t16[:, None] + LW)
    c[:, C_MS:C_MS + SC] = np.where(diag, 0.0, NEG)
    c[:, C_MS + SC:C_MS + SW] = np.where(inside, 0.0, NEG)
    c[:, C_MS0:C_MS0 + SC] = np.where(diag, 0.0, NEG)
    c[:, C_MS0 + SC:C_MS0 + SW] = np.where(w[None, :] < LW, 0.0, NEG) + np.zeros((P, 1))
    t = GROUP * (row % NG) + row // NG
    s = np.arange(P)
    c[:, C_M1:C_M1 + P] = np.where(s[None, :] > t[:, None], TAKEN, 0.0)
    te = np.maximum(t, LW - 1)[:, None]
    s = np.arange(TOPK)[None, :]
    c[:, C_M0:C_M0 + TOPK] = np.where(s > te, FUTURE, np.where(s > te - LW, TAKEN, 0.0))
    theta = (1.0 / np.float32(10000.0) ** (np.float32(2.0) * np.arange(HALF, dtype=np.float32) / np.float32(DR))).astype(np.float32)
    pos = [P * i + row for i in range(TPB)]
    pos += [p + np.maximum(p, LW - 1) - (LW - 1) for p in pos]
    pos += [LW + row % SEL]
    angle = (np.stack(pos, 1).astype(np.float32)[:, :, None] * theta).astype(np.float64)
    c[:, C_COS:C_SIN] = np.cos(angle).reshape(P, -1)
    c[:, C_SIN:C_END] = np.sin(angle).reshape(P, -1)
    return c


ORDER = {
    "PE": [("score", -1), ("turn", -2), ("index1", 2), ("key", 0), ("value", -2), ("index2", 2), ("index3", 2),
           ("score", 0), ("turn", -1), ("hid2", -2), ("query", 2), ("key", 1), ("keysT", 2), ("norm1", 3),
           ("value", -1), ("gate1", 3), ("turn", 0), ("cwin", 2), ("score", 1), ("key", 2), ("queryT0", 2),
           ("value", 0), ("hid1", 3), ("queryT1", 2), ("mix", -1), ("score", 2), ("turn", 1), ("normm", 3),
           ("key", 3), ("proj", 3), ("norm2", -1), ("value", 1), ("gate2", -1), ("index0", 3)],
    "ACT": [("index0", 2), ("turn", -2), ("score", -1), ("index1", 2), ("act2", -2), ("key", 0), ("index2", 2),
            ("weigh", -1), ("index3", 2), ("turn", -1), ("stat1", 3), ("score", 0), ("query", 2), ("norm1", 3),
            ("weigh", 0), ("key", 1), ("keysT", 2), ("gate1", 3), ("turn", 0), ("cwin", 2), ("act1", 3),
            ("score", 1), ("queryT0", 2), ("key", 2), ("weigh", 1), ("sum1", 3), ("queryT1", 2), ("normm", 3),
            ("mix", -1), ("turn", 1), ("key", 3), ("norm2", -1), ("score", 2), ("proj", 3), ("weigh", 2),
            ("krow", 3), ("gate2", -1)],
    "DVE": [("rope0", 2), ("act1", 3), ("score", 1), ("hid1", 3), ("rope1", 2), ("turn", 1), ("value", 0),
            ("sum1", 3), ("key", 3), ("normm", 3), ("mix", -1), ("key", 4), ("norm2", -1), ("score", 2),
            ("pick2", 2), ("stat1", 4), ("turn", 2), ("value", 1), ("krow", 3), ("pick3", 2), ("score", 3),
            ("act2", -1), ("index0", 3), ("key", 5), ("index1", 3), ("turn", 3), ("value", 2), ("hid2", -1),
            ("index2", 3), ("key", 6), ("index3", 3), ("score", 4), ("pick0", 3), ("sum2", -1), ("norm1", 4),
            ("turn", 4), ("pick1", 3), ("value", 3)],
    "SP": [("krow", 2), ("store", -1)],
}
AHEAD1, BEHIND = 3, -1
BY_DUO = ("key", "weigh", "score", "turn", "value")


def run_steps(engine, parts, setup=None):
    for n in range(-5, TILES + 3):
        for part, ahead in ORDER[engine]:
            duo = part in BY_DUO
            at = (ND * n if duo else n) + ahead
            if part in parts and 0 <= at < (ND * TILES if duo else TILES):
                if setup and part == "query" and at == 0:
                    setup()
                if duo:
                    parts[part](at // ND, at % ND)
                else:
                    parts[part](at)


def columns(n):
    i = n % TPB
    return TOPK if i == 0 else P * i + LW


def known(n, d):
    return n % TPB == 0 and (d + 1) * DUO <= LW


def slot(g):
    d, q, k = g // (2 * GROUP), g // GROUP % 2, g % GROUP
    return 2 * GROUP * d + 2 * k + q


def chunks(n):
    w = columns(n)
    return [(a, min(512, w - a)) for a in range(0, w, 512)]


def fills(n):
    return NI * len(chunks(n))


def fills_before(n):
    return sum(fills(m) for m in range(n))


def quarter(n, j):
    all_fills = [(h, a, w) for a, w in chunks(n) for h in range(NI)]
    k = len(all_fills) // 4
    return [(fills_before(n) + f, *all_fills[f]) for f in range(j * k, (j + 1) * k)]


def macaron_block(nc, x, w_dkv, w_uk, w_uv, w_dq, w_uq, w_qr, w_kr, w_out, iwq, iwk, iw, raw_delta,
                  w_gate, w_up, w_down, consts, out):
    with ExitStack() as ctx:
        def sb(name, shape, dt=F32):
            return ctx.enter_context(nc.sbuf_tensor(name, shape, dt))

        def bank(name):
            return ctx.enter_context(nc.psum_tensor(name, [P, 512], F32))

        def sem(name):
            return ctx.enter_context(nc.semaphore(name))

        table = nc.dram_tensor("key_table", [BATCH * LEN, KD], F32).ap()

        ps_f1, ps_f2, ps_i0, ps_i1, ps_tk, ps_tp = [
            bank(m) for m in ("ps_f1", "ps_f2", "ps_i0", "ps_i1", "ps_tk", "ps_tp")]
        ps_i = (ps_i0, ps_i1)
        ps_ss = ctx.enter_context(nc.psum_tensor("ps_ss", [P, 2, 512], F32))
        ps_s = (ps_ss[:, 0, :], ps_ss[:, 1, :])
        ps_s0, ps_s1 = ps_s
        ps_ckr = ps_i0[:, P:P + KD]

        def turned_in(k):
            return ps_i0[:, 0:P] if k == "m" else ps_f1[:, HID:512]

        cst = sb("cst", [P, C_END])
        ident = cst[:, C_ID:C_ID + P]
        wg_i = sb("wg_i", [P, HC, D], I32)
        wu_i = sb("wu_i", [P, HC, D], I32)
        wd_i = sb("wd_i", [P, HC, P], I32)
        wg_f = sb("wg_f", [P, HC, D])
        wu_f = sb("wu_f", [P, HC, D])
        wd_f = sb("wd_f", [P, HC, P])
        wgT = sb("wgT", [P, HC, P])
        wuT = sb("wuT", [P, HC, P])
        wdT = sb("wdT", [P, HC, D])
        wckr = sb("wckr", [P, KD])
        wiq = sb("wiq", [P, NI * DH])
        wik = sb("wik", [P, 2 * DH])
        iw_b = sb("iw_b", [P, NI])
        wuq_s = sb("wuq_s", [DQ, NH * DH])
        wuk_s = sb("wuk_s", [DC, NH * DH])
        wuv_s = sb("wuv_s", [DC, NH * DH])
        wdq_s = sb("wdq_s", [P, DQ])
        wout_s = sb("wout_s", [P, NH // 2, D])
        up_T = sb("up_T", [P, NH // 2, DQ + 2 * DC])
        wdqT = sb("wdqT", [DQ, P])
        wq64 = sb("wq64", [DQ, NH, KD])
        wqf = sb("wqf", [P, NH * KD])
        wvo = sb("wvo", [P, 2, D])
        delta = sb("delta", [P, 8, HALF])
        trig = sb("trig", [P, NTRIG, 4, HALF])
        trt = sb("trt", [P, 2, NTRIG, HALF])

        xs = sb("xs", [P, TILES, D])
        stats = {k: sb("stats" + k, [P, 6]) for k in "1m2"}
        mv = {k: sb("mv" + k, [P, 2]) for k in "1m2"}
        rstd = {k: sb("rstd" + k, [P, 1]) for k in "1m2"}
        rln = {k: sb("rln" + k, [P, 1]) for k in "1m2"}
        eps = sb("eps", [P, 1])
        xn = {k: sb("xn" + k, [P, D]) for k in "1m2"}
        xnT = {k: sb("xnT" + k, [P, P]) for k in "1m2"}
        x1nT = xnT["m"]
        f_abs = sb("f_abs", [P, HID])
        f_ln = sb("f_ln", [P, HID])
        f_sig = sb("f_sig", [P, HID])
        f_gu = sb("f_gu", [P, HID])
        hid = sb("hid", [P, HC, P])

        qiT = sb("qiT", [P, NI // 2, P])
        kiT = sb("kiT", [P, BATCH, LEN])
        pos_s = sb("pos_s", [P, NI, ICOLS])
        isc = sb("isc", [P, ICOLS])
        top8 = sb("top8", [P, SEL])
        idx = sb("idx", [P, SEL], U32)
        idxT = sb("idxT", [P, RING, NG], U32)

        k_abs = sb("k_abs", [P, DR])
        k_ln = sb("k_ln", [P, DR])
        rows = sb("rows", [P, RING, KD + DR])
        k_rot = sb("k_rot", [P, 2 * DR])
        krow = sb("krow", [P, 2, KD])
        keysT = sb("keysT", [P, RING, LW + P])
        c_win = sb("c_win", [WIN, RING, P // QUAD, DC])
        gath = sb("gath", [P, RING, NG, KD])
        g_rot = sb("g_rot", [P, 2 * GROUP, 2 * DR])

        q_abs = sb("q_abs", [P, NH, DR])
        q_ln = sb("q_ln", [P, NH, DR])
        q_mu = sb("q_mu", [P, NH, 2 * DR])
        q_rot = sb("q_rot", [P, NH, 2 * DR])
        qrow = sb("qrow", [P, 2, NH, KD])
        qT = sb("qT", [P, RING, 2, ND, QUAD, NH])

        kT = sb("kT", [P, 2, 512])
        sm = sb("sm", [P, 2, SW])
        nmx = sb("nmx", [P, 2])
        den = sb("den", [P, 2])
        rden = sb("rden", [P, 2])
        pr = sb("pr", [P, 2, 2, SW])
        prT = sb("prT", [P, 2, 2, SC // NH, NH])
        prTw = sb("prTw", [WIN, 2, 2, QUAD, NH])
        oT = sb("oT", [P, 2, P, 2])

        x_in = [sem("x_first_in"), sem("x_rest_in")]
        ffn_w_in = [sem("w_gate_in"), sem("w_up_in"), sem("w_down_in")]
        delta_in, ident_in = sem("delta_in"), sem("ident_in")
        cst_in, proj_w_in, lat_w_in, out_done = sem("cst_in"), sem("proj_w_in"), sem("lat_w_in"), sem("out_done")
        known_in = sem("known_rows_in")
        table_in = [sem(f"table_in{r}") for r in range(RING)]
        gathered = [[sem(f"gathered{r}_{d}") for d in range(ND)] for r in range(RING)]
        R = {m: sem(m) for m in (
            "wf", "eps", "rl1", "rlm", "rl2", "w_T", "w_Ts", "trig_e", "trig_s", "trig_a", "trig_sin", "trig_done",
            "lat_T", "lat_Ts", "lat_w", "lat_ws", "wqf_p", "wqf_s",
            "x1_down", "x1", "x2_y", "x2", "x3_down", "x3",
            "st1", "mv1", "rs1", "xn1", "xT1", "xTs1", "stm", "mvm", "rsm", "xnm", "xTm", "xTsm",
            "st2", "mv2", "rs2", "xn2", "xT2", "xTs2",
            "gu1", "ab1", "ex1", "ln1", "lsig1", "sig1", "gu_s1", "hid1",
            "gu2", "ab2", "ex2", "ln2", "lsig2", "sig2", "gu_s2", "hid2",
            "proj", "qki", "k_ab", "k_ex", "k_lnd", "rows_c", "rows_mu", "rows_all", "krot_m", "krow_done",
            "iscore", "irelu", "isum", "top", "topi", "idx_T", "idx_done",
            "qproj", "q_ab", "q_ex", "q_lnd", "q_c", "q_mud", "q_rm", "qrow_done", "qT_p", "qT_done",
            "keysT_p", "keysT_done", "cwin_p", "cwin_done",
            "g_rm", "g_done", "kT_p", "kT_done", "score", "smax", "prob", "rdend", "prob_n",
            "prT_p", "prT_done", "value", "o_done")}

        block = ctx.enter_context(nc.Block())

        @block.sync
        def _(sp):
            sp.dma_start(xs[:, 0, :], x[0, 0:P, :]).then_inc(x_in[0], 16)
            sp.dma_start(wg_i[:, :, :], w_gate.rearrange("(c p) d -> p c d", p=P)).then_inc(ffn_w_in[0], 16)
            sp.dma_start(wd_i[:, :, :], w_down.rearrange("d (c p) -> d c p", p=P)).then_inc(ffn_w_in[2], 16)
            for src, dst in ((w_dkv, wckr[:, 0:DC]), (w_kr, wckr[:, DC:KD]), (iwq, wiq[:, :]),
                             (iwk, wik[:, 0:DH]), (iwk, wik[:, DH:2 * DH])):
                sp.dma_start(dst, src).then_inc(proj_w_in, 16)
            for b in range(BATCH):
                lo = 1 if b == 0 else 0
                sp.dma_start(xs[:, b * TPB + lo:(b + 1) * TPB, :],
                             x[b, lo * P:, :].rearrange("(t p) d -> p t d", p=P)).then_inc(x_in[1], 16)

            def table_rows(n):
                sp.wait_ge(R["rows_all"], 2 * (n + 1))
                sp.wait_ge(R["rows_mu"], n + 1)
                sp.wait_ge(R["rows_c"], 2 * n + 1)
                sp.dma_start(table[n * P:(n + 1) * P, :], rows[:, n % RING, 0:KD]).then_inc(table_in[n % RING], 16)
                if n % TPB == 0:
                    known_rows(n)

            def store(n):
                sp.wait_ge(R["x3"], n + 1)
                b, i = n // TPB, n % TPB
                sp.dma_start(out[b, i * P:(i + 1) * P, :], xs[:, n, :]).then_inc(out_done, 16)

            def known_rows(n):
                sp.wait_ge(table_in[n % RING], 16 * (n // RING + 1))
                if n:
                    sp.wait_ge(R["value"], ND * (n - RING) + ND)
                for j in range(GROUP):
                    rows_in = table[n * P + LW:n * P + TOPK, :].rearrange("(p a) k -> p a k", a=1)
                    sp.dma_start(gath[j * SEL:(j + 1) * SEL, n % RING, 0:LW // GROUP, :],
                                 rows_in.to_broadcast([SEL, LW // GROUP, KD])).then_inc(known_in, 16)

            run_steps("SP", {"krow": table_rows, "store": store})
            sp.wait_ge(out_done, 16 * TILES)

        @block.gpsimd
        def _(pool):
            for n in range(TILES):
                pool.wait_ge(R["idx_done"], n + 1)
                pool.wait_ge(table_in[n % RING], 16 * (n // RING + 1))
                for g in range(LW // GROUP if n % TPB == 0 else 0, NG):
                    pool.indirect_dma_start(
                        gath[:, n % RING, slot(g), :], None, table[0:(n + 1) * P, :],
                        bass.IndirectOffsetOnAxis(ap=idxT[:, n % RING, g:g + 1], axis=0),
                    ).then_inc(gathered[n % RING][g // (2 * GROUP)], 16)

        @block.scalar
        def _(act):
            act.dma_start(delta[:, 0, :], raw_delta.rearrange("(a d) -> a d", a=1).partition_broadcast(P)).then_inc(delta_in, 16)
            act.dma_start(wu_i[:, :, :], w_up.rearrange("(c p) d -> p c d", p=P)).then_inc(ffn_w_in[1], 16)
            act.dma_start(ident, consts[:, 0:P]).then_inc(ident_in, 16)
            act.dma_start(cst[:, P:C_END], consts[:, P:C_END]).then_inc(cst_in, 16)
            act.dma_start(iw_b[:, :], iw.rearrange("(a d) -> a d", a=1).partition_broadcast(P)).then_inc(cst_in, 16)
            for src, dst in ((w_uq, wuq_s[:, :]), (w_uk, wuk_s[:, :]), (w_uv, wuv_s[:, :]), (w_dq, wdq_s[:, :]),
                             (w_out.rearrange("(c p) d -> p c d", p=P), wout_s[:, :, :]),
                             (w_qr.rearrange("q (h r) -> q h r", r=DR), wq64[:, :, DC:KD])):
                act.dma_start(dst, src).then_inc(lat_w_in, 16)

            act.wait_ge(delta_in, 16)
            nc.scalar.activation(delta[:, 1, :], delta[:, 0, :], ACT.Exp, scale=-1.0).then_inc(R["trig_e"], 1)
            act.wait_ge(R["eps"], 1)
            act.wait_ge(R["trig_a"], 1)
            nc.scalar.activation(delta[:, 5:7, :], delta[:, 3:5, :], ACT.Sin).then_inc(R["trig_sin"], 1)
            nc.scalar.preload_act_table_set("natural_log_exp_and_others")
            act.wait_ge(R["w_T"], 3)
            nc.scalar.copy(wgT[:, :, :].rearrange("p a b -> p (a b)"), ps_f1[:, 0:HID])
            nc.scalar.copy(wuT[:, :, :].rearrange("p a b -> p (a b)"), ps_f2[:, 0:HID])
            nc.scalar.copy(wdT[:, :, :].rearrange("p a b -> p (a b)"), ps_i0[:, 0:HID]).then_inc(R["w_Ts"], 1)

            def setup():
                act.wait_ge(R["lat_T"], 1)
                nc.scalar.copy(up_T[:, :, :].rearrange("p a b -> p (a b)"), ps_s0[:, :])
                nc.scalar.copy(wdqT[:, :], ps_s1[0:DQ, 0:P]).then_inc(R["lat_Ts"], 1)
                act.wait_ge(R["lat_w"], 1)
                act.wait_ge(lat_w_in, 96)
                for e in range(2):
                    q4 = (ps_tk, ps_tp)[e][0:DQ, 0:4 * DC].rearrange("p (h c) -> p h c", c=DC)
                    nc.scalar.copy(wq64[:, e::2, 0:DC], q4).then_inc(R["lat_ws"], 1)
                for e in range(2):
                    nc.scalar.copy(wvo[:, e, :], ps_s[e][:, 0:D]).then_inc(R["lat_ws"], 1)
                act.wait_ge(R["wqf_p"], 1)
                nc.scalar.copy(wqf[:, :], ps_tk[:, :]).then_inc(R["wqf_s"], 1)

            def stat(k, n):
                act.wait_ge(R["mv" + k], n + 1)
                nc.scalar.activation(rln[k][:, :], mv[k][:, 1:2], ACT.Ln, bias=eps[:, 0:1]).then_inc(R["rl" + k], 1)
                act.wait_ge(R["rl" + k], n + 1)
                nc.scalar.activation(rstd[k][:, :], rln[k][:, :], ACT.Exp, scale=-0.5).then_inc(R["rs" + k], 1)

            def turned(k):
                def part(n):
                    act.wait_ge(R["xT" + k], n + 1)
                    nc.scalar.copy(xnT[k][:, :], turned_in(k)).then_inc(R["xTs" + k], 1)
                return part

            def gate(k):
                def part(n):
                    act.wait_ge(R["gu" + k], n + 1)
                    nc.scalar.activation(f_abs[:, :], ps_f1[:, 0:HID], ACT.Abs).then_inc(R["ab" + k], 1)
                    act.wait_ge(R["ab" + k], n + 1)
                    nc.scalar.activation(f_abs[:, :], f_abs[:, :], ACT.Exp, scale=-1.0).then_inc(R["ex" + k], 1)
                    act.wait_ge(R["ex" + k], n + 1)
                    nc.scalar.activation(f_ln[:, :], f_abs[:, :], ACT.Ln, bias=1.0).then_inc(R["ln" + k], 1)
                return part

            def sigmoid(k):
                def part(n):
                    act.wait_ge(R["lsig" + k], n + 1)
                    nc.scalar.activation(f_sig[:, :], f_sig[:, :], ACT.Exp).then_inc(R["sig" + k], 1)
                return part

            def proj(n):
                b, i, r = n // TPB, n % TPB, n % RING
                act.wait_ge(R["proj"], n + 1)
                for c in range(NI // 2):
                    nc.scalar.copy(qiT[:, c, :].rearrange("p (j g) -> p g j", j=GROUP),
                                   ps_i1[:, c * P:(c + 1) * P].rearrange("p (g j) -> p g j", j=GROUP))
                nc.scalar.copy(kiT[:, b, i * P:(i + 1) * P], ps_i1[:, 2 * P:3 * P]).then_inc(R["qki"], 1)
                nc.scalar.activation(k_abs[:, :], ps_ckr[:, DC:KD], ACT.Abs).then_inc(R["k_ab"], 1)
                nc.scalar.copy(rows[:, r, 0:DC], ps_ckr[:, 0:DC]).then_inc(R["rows_c"], 1)
                act.wait_ge(R["k_ab"], n + 1)
                nc.scalar.activation(k_abs[:, :], k_abs[:, :], ACT.Exp, scale=-1.0).then_inc(R["k_ex"], 1)
                act.wait_ge(R["k_ex"], n + 1)
                nc.scalar.activation(k_ln[:, :], k_abs[:, :], ACT.Ln, bias=1.0).then_inc(R["k_lnd"], 1)

            def index(j):
                def part(n):
                    for f, h, a, w in quarter(n, j):
                        act.wait_ge(R["iscore"], f + 1)
                        nc.scalar.activation(pos_s[:, h, a:a + w], ps_i[1 - h % 2][:, 0:w], ACT.Relu).then_inc(R["irelu"], 1)
                return part

            def krow_c(n):
                src = rows[:, n % RING, 0:DC]
                act.wait_ge(R["rows_c"], 2 * n + 1)
                nc.scalar.copy(krow[:, 0, 0:DC], src)
                nc.scalar.copy(krow[:, 1, 0:DC], src).then_inc(R["rows_c"], 1)

            def query(n):
                act.wait_ge(R["qproj"], n + 1)
                q = ps_i0[:, :].rearrange("p (h k) -> p h k", k=KD)
                nc.scalar.activation(q_abs[:, :, :], q[:, :, DC:KD], ACT.Abs).then_inc(R["q_ab"], 1)
                nc.scalar.copy(qrow[:, 0, :, 0:DC], q[:, :, 0:DC])
                act.wait_ge(R["q_ab"], n + 1)
                nc.scalar.activation(q_abs[:, :, :], q_abs[:, :, :], ACT.Exp, scale=-1.0).then_inc(R["q_ex"], 1)
                nc.scalar.copy(qrow[:, 1, :, 0:DC], q[:, :, 0:DC]).then_inc(R["q_c"], 1)
                act.wait_ge(R["q_ex"], n + 1)
                nc.scalar.activation(q_ln[:, :, :], q_abs[:, :, :], ACT.Ln, bias=1.0).then_inc(R["q_lnd"], 1)

            def keys_turned(n):
                act.wait_ge(R["keysT_p"], n + 1)
                if n % TPB < TPB - 1:
                    nc.scalar.copy(keysT[:, (n + 1) % RING, 0:LW], ps_i1[:, P - LW:P])
                nc.scalar.copy(keysT[:, n % RING, LW:LW + P], ps_i1[:, 0:P]).then_inc(R["keysT_done"], 1)

            def queryT(v):
                def part(n):
                    r = n % RING
                    act.wait_ge(R["qT_p"], 2 * n + v + 1)
                    for e in range(2):
                        src = ps_i[v][e * KD:(e + 1) * KD, :].rearrange("k (h d q t) -> k q d h t", h=NH // 2, q=2, t=QUAD)
                        for par in range(2):
                            for d in range(ND):
                                dst = qT[par * KD:(par + 1) * KD, r, v, d, :, e::2].rearrange("k t h -> k h t")
                                last = nc.scalar.copy(dst, src[:, par, d])
                    last.then_inc(R["qT_done"], 1)
                return part

            def cwin(n):
                act.wait_ge(R["cwin_p"], n + 1)
                nc.scalar.copy(c_win[:, n % RING, :, :].rearrange("p q c -> p (q c)"),
                               ps_i1[0:WIN, P:P + (P // QUAD) * DC]).then_inc(R["cwin_done"], 1)

            def key(n, d):
                k = n * ND + d
                act.wait_ge(R["kT_p"], k + 1)
                nc.scalar.copy(kT[:, k % 2, :], ps_tk[:, :]).then_inc(R["kT_done"], 1)

            def score(n, d):
                k = n * ND + d
                act.wait_ge(R["smax"], k + 1)
                for q in range(2):
                    last = nc.scalar.activation(pr[:, k % 2, q, :], sm[:, q, :], ACT.Exp, bias=nmx[:, q:q + 1],
                                                scale=-1.0, accum_out=den[:, q:q + 1])
                last.then_inc(R["prob"], 1)

            def weigh(n, d):
                k = n * ND + d
                act.wait_ge(R["rdend"], k + 1)
                for q in range(2):
                    last = nc.scalar.activation(pr[:, k % 2, q, :], pr[:, k % 2, q, :], ACT.Copy, scale=rden[:, q:q + 1])
                last.then_inc(R["prob_n"], 1)

            def turn(n, d):
                k = n * ND + d
                act.wait_ge(R["prT_p"], k + 1)
                nc.scalar.copy(prT[:, k % 2].rearrange("p q t h -> p (q t h)"), ps_tp[:, 0:2 * SC])
                nc.scalar.copy(prTw[:, k % 2].rearrange("p q t h -> p (q t h)"),
                               ps_tp[0:WIN, 2 * SC:512]).then_inc(R["prT_done"], 1)

            run_steps("ACT", {"stat1": lambda n: stat("1", n), "norm1": turned("1"), "gate1": gate("1"), "act1": sigmoid("1"),
                       "sum1": lambda n: stat("m", n), "normm": turned("m"), "proj": proj,
                       **{f"index{j}": index(j) for j in range(4)},
                       "krow": krow_c, "query": query, "keysT": keys_turned, "cwin": cwin, "queryT0": queryT(0), "queryT1": queryT(1),
                       "key": key, "score": score, "weigh": weigh, "turn": turn, "mix": lambda n: stat("2", n),
                       "norm2": turned("2"), "gate2": gate("2"), "act2": sigmoid("2")}, setup)

        @block.vector
        def _(dve):
            nc.vector.memset(eps[:, :], EPS).then_inc(R["eps"], 1)
            for k, (src, dst) in enumerate(((wg_i, wg_f), (wu_i, wu_f), (wd_i, wd_f))):
                dve.wait_ge(ffn_w_in[k], 16)
                nc.vector.tensor_scalar(dst[:, :, :], src[:, :, :], WSCALE, None, ALU.mult).then_inc(R["wf"], 1)
            pi = float(np.pi)
            top = 3.1415925
            dve.wait_ge(R["trig_e"], 1)
            nc.vector.tensor_scalar(delta[:, 2, :], delta[:, 1, :], 1.0, None, ALU.add).then_inc(R["trig_s"], 1)
            dve.wait_ge(R["trig_s"], 1)
            nc.vector.reciprocal(delta[:, 2, :], delta[:, 2, :]).then_inc(R["trig_s"], 1)
            dve.wait_ge(R["trig_s"], 2)
            nc.vector.tensor_scalar(delta[:, 3, :], delta[:, 2, :], pi, None, ALU.mult)
            nc.vector.tensor_scalar(delta[:, 4, :], delta[:, 2, :], -2.0 * pi, pi, ALU.mult, ALU.add).then_inc(R["trig_s"], 1)
            dve.wait_ge(R["trig_s"], 3)
            nc.vector.tensor_scalar(delta[:, 3:5, :], delta[:, 3:5, :], top, -top, ALU.min, ALU.max).then_inc(R["trig_a"], 1)

            def trig_tables():
                done = 0
                cd, sd = delta[:, 7:8, :], delta[:, 6:7, :]
                dve.wait_ge(R["trig_sin"], 1)
                nc.vector.tensor_tensor(delta[:, 7, :], delta[:, 5, :], delta[:, 5, :], ALU.mult).then_inc(R["trig_s"], 1)
                dve.wait_ge(R["trig_s"], 4)
                nc.vector.tensor_scalar(delta[:, 7, :], delta[:, 7, :], -2.0, 1.0, ALU.mult, ALU.add).then_inc(R["trig_s"], 1)
                dve.wait_ge(R["trig_s"], 5)
                dve.wait_ge(cst_in, 32)
                cb = cst[:, C_COS:C_SIN].rearrange("p (n f) -> p n f", f=HALF)
                sn = cst[:, C_SIN:C_END].rearrange("p (n f) -> p n f", f=HALF)
                full = [P, NTRIG, HALF]
                for j, (u, v, op) in enumerate(((cb, sn, ALU.add), (sn, cb, ALU.subtract))):
                    nc.vector.tensor_tensor(trt[:, 0, :, :], u, cd.to_broadcast(full), ALU.mult)
                    nc.vector.tensor_tensor(trt[:, 1, :, :], v, sd.to_broadcast(full), ALU.mult).then_inc(R["trig_s"], 1)
                    dve.wait_ge(R["trig_s"], 6 + 2 * j)
                    dst = trig[:, :, 0, :] if j == 0 else trig[:, :, 3, :]
                    nc.vector.tensor_tensor(dst, trt[:, 0, :, :], trt[:, 1, :, :], op).then_inc(R["trig_s"], 1)
                    dve.wait_ge(R["trig_s"], 7 + 2 * j)
                nc.vector.tensor_copy(trig[:, :, 1, :], trig[:, :, 0, :])
                nc.vector.tensor_scalar(trig[:, :, 2, :], trig[:, :, 3, :], -1.0, None, ALU.mult).then_inc(R["trig_done"], 1)
                dve.wait_ge(R["trig_done"], 1)

            def stat(k, n):
                nc.vector.bn_stats(stats[k][:, :], xs[:, n, :]).then_inc(R["st" + k], 1)
                dve.wait_ge(R["st" + k], n + 1)
                nc.vector.bn_aggr(mv[k][:, :], stats[k][:, :]).then_inc(R["mv" + k], 1)

            def normed(k):
                def part(n):
                    dve.wait_ge(R["rs" + k], n + 1)
                    nc.vector.tensor_scalar(xn[k][:, :], xs[:, n, :], mv[k][:, 0:1], rstd[k][:, 0:1], ALU.subtract,
                                            ALU.mult).then_inc(R["xn" + k], 1)
                    if k == "1" and n == 0:
                        trig_tables()
                return part

            def stat1(n):
                dve.wait_ge(x_in[min(n, 1)], 16 if n == 0 else 32)
                stat("1", n)

            def log_sigmoid(k):
                def part(n):
                    dve.wait_ge(R["ln" + k], n + 1)
                    nc.vector.scalar_tensor_tensor(f_sig[:, :], ps_f1[:, 0:HID], 0.0, f_ln[:, :],
                                                   ALU.min, ALU.subtract).then_inc(R["lsig" + k], 1)
                return part

            def hidden(k):
                def part(n):
                    dve.wait_ge(R["sig" + k], n + 1)
                    nc.vector.tensor_tensor(f_gu[:, :], ps_f1[:, 0:HID], f_sig[:, :], ALU.mult).then_inc(R["gu_s" + k], 1)
                    dve.wait_ge(R["gu_s" + k], n + 1)
                    nc.vector.tensor_tensor(hid[:, :, :].rearrange("p a b -> p (a b)"), ps_f2[:, 0:HID], f_gu[:, :],
                                            ALU.mult).then_inc(R["hid" + k], 1)
                return part

            def sum1(n):
                dve.wait_ge(R["x1_down"], n + 1)
                nc.vector.scalar_tensor_tensor(xs[:, n, :], ps_f2[:, HID:512], 0.5, xs[:, n, :],
                                               ALU.mult, ALU.add).then_inc(R["x1"], 1)
                dve.wait_ge(R["x1"], n + 1)
                stat("m", n)

            def krow_rot(n):
                i, r = n % TPB, n % RING
                dve.wait_ge(R["k_lnd"], n + 1)
                for dst, a in ((DC, 0), (DC + DR, HALF), (DC + DR + HALF, 0)):
                    w = DR if dst == DC else HALF
                    ins = nc.vector.scalar_tensor_tensor(rows[:, r, dst:dst + w], ps_ckr[:, DC + a:DC + a + w], 0.0,
                                                         k_ln[:, a:a + w], ALU.max, ALU.add)
                    ins.then_inc(R["rows_mu"] if dst == DC else R["rows_all"], 1)
                dve.wait_ge(R["rows_all"], 2 * (n + 1))
                dve.wait_ge(R["rows_mu"], n + 1)
                nc.vector.tensor_tensor(k_rot[:, :], rows[:, r, DC:KD + DR], trig[:, i, :, :].rearrange("p a f -> p (a f)"),
                                        ALU.mult).then_inc(R["krot_m"], 1)
                dve.wait_ge(R["krot_m"], n + 1)
                for c in range(2):
                    nc.vector.tensor_tensor(krow[:, c, DC:KD], k_rot[:, 0:DR], k_rot[:, DR:2 * DR],
                                            ALU.add).then_inc(R["krow_done"], 1)

            def index(j):
                def part(n):
                    for f, h, a, w in quarter(n, j):
                        dve.wait_ge(R["irelu"], f + 1)
                        dst = isc[:, a:a + w]
                        if h == 0:
                            ins = nc.vector.tensor_scalar(dst, pos_s[:, 0, a:a + w], iw_b[:, 0:1], None, ALU.mult)
                        else:
                            dve.wait_ge(R["isum"], f + n)
                            ins = nc.vector.scalar_tensor_tensor(dst, pos_s[:, h, a:a + w], iw_b[:, h:h + 1], dst,
                                                                 ALU.mult, ALU.add)
                        ins.then_inc(R["isum"], 1)
                    if j == 3:
                        index_masks(n)
                return part

            def index_masks(n):
                i = n % TPB
                m = cst[:, C_M0:C_M0 + TOPK] if i == 0 else cst[:, C_M1:C_M1 + P]
                w = columns(n)
                dst = isc[:, w - m.shape[1]:w]
                s = fills_before(n + 1) + n
                dve.wait_ge(R["isum"], s)
                nc.vector.tensor_tensor(dst, dst, m, ALU.add).then_inc(R["isum"], 1)
                dve.wait_ge(R["isum"], s + 1)

            def pick(k):
                def part(n):
                    if n:
                        pick_eight(n, k)
                    elif k == 0:
                        for j in range(4):
                            pick_eight(0, j)
                return part

            def pick_eight(n, k):
                w, e = columns(n), slice(8 * k, 8 * k + 8)
                base = 7 * n + 2 * k
                nc.vector.max(top8[:, e], isc[:, 0:w]).then_inc(R["top"], 1)
                dve.wait_ge(R["top"], base + 1)
                nc.vector.max_index(idx[:, e], top8[:, e], isc[:, 0:w]).then_inc(R["topi"], 1)
                if k < 3:
                    nc.vector.match_replace(isc[:, 0:w], top8[:, e], isc[:, 0:w], TAKEN).then_inc(R["top"], 1)
                    dve.wait_ge(R["top"], base + 2)
                else:
                    dve.wait_ge(R["topi"], 4 * n + 4)
                    r = n % RING
                    if n < TPB:
                        nc.vector.transpose(idxT[:, r, :], idx[:, :]).then_inc(R["idx_done"], 1)
                    else:
                        nc.vector.transpose(idxT[:, r, :], idx[:, :]).then_inc(R["idx_T"], 1)
                        dve.wait_ge(R["idx_T"], n - TPB + 1)
                        nc.vector.tensor_scalar(idxT[:, r, :], idxT[:, r, :], float(LEN), None, ALU.add).then_inc(R["idx_done"], 1)

            def rope0(n):
                q = ps_i0[:, :].rearrange("p (h k) -> p h k", k=KD)
                dve.wait_ge(R["q_lnd"], n + 1)
                for dst, a in ((0, 0), (DR, HALF), (DR + HALF, 0)):
                    w = DR if dst == 0 else HALF
                    nc.vector.scalar_tensor_tensor(q_mu[:, :, dst:dst + w], q[:, :, DC + a:DC + a + w], 0.0,
                                                   q_ln[:, :, a:a + w], ALU.max, ALU.add).then_inc(R["q_mud"], 1)
                dve.wait_ge(R["q_mud"], 3 * (n + 1))
                rope(n, 0)

            def rope1(n):
                dve.wait_ge(R["qrow_done"], 2 * n + 1)
                rope(n, 1)

            def rope(n, v):
                    i = n % TPB
                    tr = trig[:, i + v * TPB, :, :].rearrange("p (o a) f -> p o (a f)", o=1).to_broadcast([P, NH, 2 * DR])
                    nc.vector.tensor_tensor(q_rot[:, :, :], q_mu[:, :, :], tr, ALU.mult).then_inc(R["q_rm"], 1)
                    dve.wait_ge(R["q_rm"], 2 * n + v + 1)
                    nc.vector.tensor_tensor(qrow[:, v, :, DC:KD], q_rot[:, :, 0:DR], q_rot[:, :, DR:2 * DR],
                                            ALU.add).then_inc(R["qrow_done"], 1)

            def key(n, d):
                r, k = n % RING, n * ND + d
                if known(n, d):
                    dve.wait_ge(known_in, 16 * GROUP * (n // TPB + 1))
                else:
                    times = sum(1 for m in range(r, n + 1, RING) if not known(m, d))
                    dve.wait_ge(gathered[r][d], 16 * 2 * GROUP * times)
                gs = slice(2 * GROUP * d, 2 * GROUP * (d + 1))
                tr = trig[:, RANKS, :, :].rearrange("p (o a) f -> p o (a f)", o=1).to_broadcast([P, 2 * GROUP, 2 * DR])
                mu = gath[:, r, gs, DC:KD]
                if k:
                    dve.wait_ge(R["g_done"], k)
                nc.vector.tensor_tensor(g_rot[:, :, 0:DR], mu, tr[:, :, 0:DR], ALU.mult)
                nc.vector.tensor_tensor(g_rot[:, :, DR:DR + HALF], mu[:, :, HALF:DR], tr[:, :, DR:DR + HALF], ALU.mult)
                nc.vector.tensor_tensor(g_rot[:, :, DR + HALF:2 * DR], mu[:, :, 0:HALF], tr[:, :, DR + HALF:2 * DR],
                                        ALU.mult).then_inc(R["g_rm"], 1)
                dve.wait_ge(R["g_rm"], k + 1)
                nc.vector.tensor_tensor(gath[:, r, gs, DC:KD], g_rot[:, :, 0:DR], g_rot[:, :, DR:2 * DR],
                                        ALU.add).then_inc(R["g_done"], 1)

            def score(n, d):
                k = n * ND + d
                dve.wait_ge(R["score"], k + 1)
                for q in range(2):
                    first = n % TPB == 0 and 2 * d + q < LW // QUAD
                    m = cst[:, C_MS0:C_MS0 + SW] if first else cst[:, C_MS:C_MS + SW]
                    last = nc.vector.tensor_tensor_reduce(sm[:, q, :], ps_s[q][:, 0:SW], m, -SCALE, 3.0e38, ALU.add,
                                                          ALU.min, nmx[:, q:q + 1])
                last.then_inc(R["smax"], 1)

            def turn(n, d):
                k = n * ND + d
                dve.wait_ge(R["prob"], k + 1)
                nc.vector.reciprocal(rden[:, :], den[:, :]).then_inc(R["rdend"], 1)

            def value(n, d):
                k = n * ND + d
                dve.wait_ge(R["value"], k + 1)
                nc.vector.tensor_copy(oT[:, n % 2, d * DUO:(d + 1) * DUO, :].rearrange("c (q t) h -> c q (t h)", q=2),
                                      ps_ss[:, :, 256:256 + 2 * QUAD]).then_inc(R["o_done"], 1)

            def mix(n):
                dve.wait_ge(R["x2_y"], n + 1)
                nc.vector.tensor_tensor(xs[:, n, :], ps_f2[:, HID:512], xs[:, n, :], ALU.add).then_inc(R["x2"], 1)
                dve.wait_ge(R["x2"], n + 1)
                stat("2", n)

            def sum2(n):
                dve.wait_ge(R["x3_down"], n + 1)
                nc.vector.scalar_tensor_tensor(xs[:, n, :], ps_f2[:, HID:512], 0.5, xs[:, n, :],
                                               ALU.mult, ALU.add).then_inc(R["x3"], 1)

            run_steps("DVE", {"stat1": stat1, "norm1": normed("1"), "act1": log_sigmoid("1"), "hid1": hidden("1"),
                       "sum1": sum1, "normm": normed("m"), "krow": krow_rot,
                       **{f"index{j}": index(j) for j in range(4)}, "pick0": pick(0), "pick1": pick(1),
                       "pick2": pick(2), "pick3": pick(3), "rope0": rope0, "rope1": rope1, "key": key, "score": score, "turn": turn,
                       "value": value, "mix": mix, "norm2": normed("2"), "act2": log_sigmoid("2"), "hid2": hidden("2"),
                       "sum2": sum2})

        @block.tensor
        def _(pe):
            pe.wait_ge(ident_in, 16)
            for k, (src, dst) in enumerate(((wg_f, ps_f1), (wu_f, ps_f2), (wd_f, ps_i0))):
                pe.wait_ge(R["wf"], k + 1)
                for c in range(HC):
                    last = nc.tensor.transpose(dst[:, c * P:(c + 1) * P], src[:, c, :], ident)
                last.then_inc(R["w_T"], 1)

            def setup():
                pe.wait_ge(lat_w_in, 96)
                for c in range(NH // 2):
                    cols = slice(c * P, (c + 1) * P)
                    nc.tensor.transpose(ps_s0[:, c * P:c * P + DQ], wuq_s[:, cols], ident[0:DQ, 0:DQ])
                    nc.tensor.transpose(ps_s0[:, c * P + DQ:c * P + DQ + DC], wuk_s[:, cols], ident[0:DC, 0:DC])
                    nc.tensor.transpose(ps_s0[:, c * P + DQ + DC:(c + 1) * P], wuv_s[:, cols], ident[0:DC, 0:DC])
                nc.tensor.transpose(ps_s1[0:DQ, 0:P], wdq_s[:, :], ident).then_inc(R["lat_T"], 1)
                pe.wait_ge(R["lat_Ts"], 1)
                for h in range(NH):
                    e, c = h % 2, h // 2
                    rows_h = slice(e * DH, (e + 1) * DH)
                    nc.tensor.matmul((ps_tk, ps_tp)[e][0:DQ, c * DC:(c + 1) * DC], up_T[rows_h, c, 0:DQ],
                                     up_T[rows_h, c, DQ:DQ + DC], start=True, stop=True)
                    last = nc.tensor.matmul(ps_s[e][c * DC:(c + 1) * DC, 0:D], up_T[rows_h, c, DQ + DC:DQ + 2 * DC],
                                            wout_s[rows_h, c, :], start=True, stop=True)
                last.then_inc(R["lat_w"], 1)
                pe.wait_ge(R["lat_ws"], 4)
                nc.tensor.matmul(ps_tk[:, :], wdqT[:, :], wq64[:, :, :].rearrange("p h k -> p (h k)"),
                                 start=True, stop=True).then_inc(R["wqf_p"], 1)
                pe.wait_ge(R["wqf_s"], 1)

            def turned(k):
                def part(n):
                    if n == 0 and k == "1":
                        pe.wait_ge(R["w_Ts"], 1)
                    if k == "m" and n:
                        pe.wait_ge(R["qT_done"], 2 * n - 1)
                    if k == "1" and n > AHEAD1 - BEHIND:
                        pe.wait_ge(R["gu_s2"], n - (AHEAD1 - BEHIND))
                    elif k == "1" and n:
                        pe.wait_ge(R["gu_s1"], n)
                    pe.wait_ge(R["xn" + k], n + 1)
                    nc.tensor.transpose(turned_in(k), xn[k][:, :], ident).then_inc(R["xT" + k], 1)
                return part

            def gate_up(k, n):
                if k == "1" and n > AHEAD1 - BEHIND:
                    pe.wait_ge(R["x3"], n - (AHEAD1 - BEHIND))
                elif k == "1" and n:
                    pe.wait_ge(R["x1"], n)
                pe.wait_ge(R["xTs" + k], n + 1)
                for w, dst in ((wgT, ps_f1), (wuT, ps_f2)):
                    for c in range(HC):
                        last = nc.tensor.matmul(dst[:, c * P:(c + 1) * P], w[:, c, :], xnT[k][:, :], start=True, stop=True)
                last.then_inc(R["gu" + k], 1)

            def down(k, n):
                pe.wait_ge(R["hid" + k], n + 1)
                for c in range(HC):
                    last = nc.tensor.matmul(ps_f2[:, HID:512], hid[:, c, :], wdT[:, c, :], start=(c == 0), stop=(c == HC - 1))
                last.then_inc(R["x1_down" if k == "1" else "x3_down"], 1)

            def proj(n):
                if n == 0:
                    pe.wait_ge(proj_w_in, 80)
                pe.wait_ge(R["xTsm"], n + 1)
                if n:
                    pe.wait_ge(R["qT_done"], 2 * n)
                for c in range(NI // 2):
                    nc.tensor.matmul(ps_i1[:, c * P:(c + 1) * P], wiq[:, c * P:(c + 1) * P], x1nT[:, :], start=True, stop=True)
                nc.tensor.matmul(ps_i1[:, 2 * P:3 * P], wik[:, :], x1nT[:, :], start=True, stop=True)
                nc.tensor.matmul(ps_ckr, x1nT[:, :], wckr[:, :], start=True, stop=True).then_inc(R["proj"], 1)

            def index(j):
                def part(n):
                    b = n // TPB
                    for f, h, a, w in quarter(n, j):
                        e = h % 2
                        if f - fills_before(n) >= 2:
                            pe.wait_ge(R["irelu"], f - 1)
                        elif h == 0:
                            pe.wait_ge(R["qki"], n + 1)
                        else:
                            pe.wait_ge(R["rows_all"], 2 * (n + 1))
                        q = qiT[e * DH:(e + 1) * DH, h // 2, :]
                        nc.tensor.matmul(ps_i[1 - e][:, 0:w], q, kiT[e * DH:(e + 1) * DH, b, a:a + w],
                                         start=True, stop=True).then_inc(R["iscore"], 1)
                return part

            def query(n):
                pe.wait_ge(R["irelu"], fills_before(n + 1))
                nc.tensor.matmul(ps_i0[:, :], x1nT[:, :], wqf[:, :], start=True, stop=True).then_inc(R["qproj"], 1)

            def keys_turned(n):
                pe.wait_ge(R["krow_done"], 2 * (n + 1))
                pe.wait_ge(R["rows_c"], 2 * (n + 1))
                nc.tensor.transpose(ps_i1[:, 0:P], krow[:, :, :].rearrange("p a b -> p (a b)"), ident).then_inc(R["keysT_p"], 1)

            def queryT(v):
                def part(n):
                    pe.wait_ge(R["q_c"], n + 1)
                    pe.wait_ge(R["qrow_done"], 2 * n + v + 1)
                    if v == 1:
                        pe.wait_ge(R["cwin_done"], n + 1)
                    for c in range(NH // 2):
                        last = nc.tensor.transpose(ps_i[v][:, c * P:(c + 1) * P],
                                                   qrow[:, v, 2 * c:2 * c + 2, :].rearrange("p a b -> p (a b)"), ident)
                    last.then_inc(R["qT_p"], 1)
                return part

            def cwin(n):
                r = n % RING
                pe.wait_ge(R["keysT_done"], n + 1)
                for q in range(P // QUAD):
                    a = window(n, q)
                    last = nc.tensor.transpose(ps_i1[0:WIN, P + q * DC:P + (q + 1) * DC], keysT[0:DC, r, a:a + WIN], ident[0:DC, 0:DC])
                last.then_inc(R["cwin_p"], 1)

            def window(n, q):
                return max(QUAD * q, LW) if n % TPB == 0 else QUAD * q

            def key(n, d):
                r, k = n % RING, n * ND + d
                pe.wait_ge(R["g_done"], k + 1)
                if k:
                    pe.wait_ge(R["kT_done"], k)
                for g in range(GROUP):
                    a = slot(2 * GROUP * d + g)
                    pair = gath[:, r, a:a + 2, :].rearrange("p a k -> p (a k)")
                    last = nc.tensor.transpose(ps_tk[:, g * P:(g + 1) * P], pair, ident)
                last.then_inc(R["kT_p"], 1)

            def score(n, d):
                r, k = n % RING, n * ND + d
                pe.wait_ge(R["kT_done"], k + 1)
                pe.wait_ge(R["qT_done"], 2 * (n + 1))
                if k > 1:
                    pe.wait_ge(R["o_done"], k - 1)
                if k:
                    pe.wait_ge(R["smax"], k)
                for q in range(2):
                    half = slice(q * KD, (q + 1) * KD)
                    a = window(n, 2 * d + q)
                    nc.tensor.matmul(ps_s[q][:, SC:SW], qT[half, r, 1, d, :, :].rearrange("k t h -> k (t h)"),
                                     keysT[half, r, a:a + WIN], start=True, stop=True)
                    for g in range(GROUP):
                        last = nc.tensor.matmul(
                            ps_s[q][g * SEL:(g + 1) * SEL, 0:SC],
                            qT[half, r, 0, d, g * GROUP:(g + 1) * GROUP, :].rearrange("k t h -> k (t h)"),
                            kT[half, k % 2, g * P:(g + 1) * P], start=True, stop=True)
                last.then_inc(R["score"], 1)

            def turn(n, d):
                k = n * ND + d
                pe.wait_ge(R["prob_n"], k + 1)
                if k:
                    pe.wait_ge(R["prT_done"], k)
                for q in range(2):
                    nc.tensor.transpose(ps_tp[:, q * P:(q + 1) * P], pr[:, k % 2, q, 0:SC], ident)
                    last = nc.tensor.transpose(ps_tp[0:WIN, (2 + q) * P:(3 + q) * P], pr[:, k % 2, q, SC:SW], ident)
                last.then_inc(R["prT_p"], 1)

            def value(n, d):
                r, k = n % RING, n * ND + d
                pe.wait_ge(R["prT_done"], k + 1)
                pe.wait_ge(R["cwin_done"], n + 1)
                pe.wait_ge(R["smax"], min(k + 2, ND * TILES))
                if k == ND * TILES - 1:
                    pe.wait_ge(R["o_done"], k)
                for q in range(2):
                    for j in range(NH // 2):
                        nc.tensor.matmul(ps_s[q][j * DC:(j + 1) * DC, 256:256 + 2 * QUAD], c_win[:, r, 2 * d + q, :],
                                         prTw[:, k % 2, q, :, 2 * j:2 * j + 2],
                                         start=True, stop=False, skip_group_check=True)
                    for g in range(GROUP):
                        o = 256 + 2 * GROUP * g
                        for j in range(NH // 2):
                            last = nc.tensor.matmul(
                                ps_s[q][j * DC:(j + 1) * DC, o:o + 2 * GROUP],
                                gath[:, r, slot(2 * GROUP * d + GROUP * q + g), 0:DC],
                                prT[:, k % 2, q, g * GROUP:(g + 1) * GROUP, 2 * j:2 * j + 2],
                                start=False, stop=(g == GROUP - 1), skip_group_check=True)
                last.then_inc(R["value"], 1)

            def mix(n):
                pe.wait_ge(R["o_done"], ND * (n + 1))
                if n + AHEAD1 - BEHIND < TILES:
                    pe.wait_ge(R["x1"], n + AHEAD1 - BEHIND + 1)
                else:
                    pe.wait_ge(R["x1"], TILES)
                    pe.wait_ge(R["x3"], n)
                for e in range(2):
                    last = nc.tensor.matmul(ps_f2[:, HID:512], oT[:, n % 2, :, e], wvo[:, e, :], start=(e == 0), stop=(e == 1))
                last.then_inc(R["x2_y"], 1)

            run_steps("PE", {"norm1": turned("1"), "gate1": lambda n: gate_up("1", n), "hid1": lambda n: down("1", n),
                       "normm": turned("m"), "proj": proj, **{f"index{j}": index(j) for j in range(4)}, "query": query, "keysT": keys_turned,
                       "cwin": cwin, "queryT0": queryT(0), "queryT1": queryT(1), "key": key, "score": score, "turn": turn, "value": value,
                       "mix": mix, "norm2": turned("2"), "gate2": lambda n: gate_up("2", n),
                       "hid2": lambda n: down("2", n)}, setup)


_INS = ['L0_attn_x', 'L0_attn_W_dkv', 'L0_attn_W_uk', 'L0_attn_W_uv', 'L0_attn_W_dq', 'L0_attn_W_uq', 'L0_attn_W_qr',
        'L0_attn_W_kr', 'L0_attn_W_out', 'L0_attn_idx_wq', 'L0_attn_idx_wk', 'L0_attn_idx_w', 'L0_attn_raw_delta',
        'L0_ffn_w_gate', 'L0_ffn_w_up', 'L0_ffn_w_down']


def kernel(**inputs):
    import concourse.bacc as _bacc
    from concourse.bass_utils import run_bass_kernel_spmd as _run

    nc = _bacc.Bacc("TRN2", target_bir_lowering=False, num_devices=1)
    arrays, args = {}, []
    for name in _INS + ["shape_constants"]:
        a = shape_constants() if name == "shape_constants" else np.ascontiguousarray(inputs[name])
        arrays[f"in_{name}"] = a
        args.append(nc.dram_tensor(f"in_{name}", a.shape, mybir.dt.from_np(a.dtype), kind="ExternalInput").ap())
    out = nc.dram_tensor("out_0", (BATCH, LEN, D), F32, kind="ExternalOutput").ap()
    macaron_block(nc, *args, out)
    r = _run(nc, [arrays], core_ids=[0])
    return r.results[0]["out_0"]
```

```python
from contextlib import ExitStack

import numpy as np

import concourse.bass as bass
from concourse import mybir

ALU = mybir.AluOpType
ACT = mybir.ActivationFunctionType
F32 = mybir.dt.float32
I32 = mybir.dt.int32
U32 = mybir.dt.uint32

P = 128
BATCH, LEN = 2, 1024
D = 128
HID = 384
HC = HID // P
NH, DH = 8, 64
DC, DR, DQ = 32, 32, 64
HALF = DR // 2
NI = 4
TOPK, LW = 96, 64
SEL = TOPK - LW
KD = DC + DR

TPB = LEN // P
TILES = BATCH * TPB
RING = 4
WIN = 80
GROUP = P // SEL
QUAD = 16
NG = P // GROUP
OUT = 256
DUO = 2 * QUAD
ND = P // DUO
SC = SEL * GROUP
SW = SC + WIN
ICOLS = LEN - LW
SCALE = float(KD + DR) ** -0.5
WSCALE = 1.0 / 127.0
NEG = -1.0e30
FUTURE = -1.0e38
TAKEN = -3.0e38
EPS = 1e-5
NTRIG = 2 * TPB + 1
RANKS = 2 * TPB

C_ID = 0
C_MS = C_ID + P
C_MS0 = C_MS + SW
C_M1 = C_MS0 + SW
C_M0 = C_M1 + P
C_COS = C_M0 + TOPK
C_SIN = C_COS + NTRIG * HALF
C_END = C_SIN + NTRIG * HALF


def shape_constants():
    c = np.zeros((P, C_END), np.float32)
    c[:, C_ID:C_ID + P] = np.eye(P)
    row = np.arange(P)
    t16 = row // NH
    col = np.arange(SC)
    diag = (t16[:, None] % GROUP) == (col[None, :] // SEL)
    w = np.arange(WIN)
    inside = (w[None, :] >= t16[:, None] + 1) & (w[None, :] <= t16[:, None] + LW)
    c[:, C_MS:C_MS + SC] = np.where(diag, 0.0, NEG)
    c[:, C_MS + SC:C_MS + SW] = np.where(inside, 0.0, NEG)
    c[:, C_MS0:C_MS0 + SC] = np.where(diag, 0.0, NEG)
    c[:, C_MS0 + SC:C_MS0 + SW] = np.where(w[None, :] < LW, 0.0, NEG) + np.zeros((P, 1))
    t = GROUP * (row % NG) + row // NG
    s = np.arange(P)
    c[:, C_M1:C_M1 + P] = np.where(s[None, :] > t[:, None], TAKEN, 0.0)
    te = np.maximum(t, LW - 1)[:, None]
    s = np.arange(TOPK)[None, :]
    c[:, C_M0:C_M0 + TOPK] = np.where(s > te, FUTURE, np.where(s > te - LW, TAKEN, 0.0))
    theta = (1.0 / np.float32(10000.0) ** (np.float32(2.0) * np.arange(HALF, dtype=np.float32) / np.float32(DR))).astype(np.float32)
    pos = [P * i + row for i in range(TPB)]
    pos += [p + np.maximum(p, LW - 1) - (LW - 1) for p in pos]
    pos += [LW + row % SEL]
    angle = (np.stack(pos, 1).astype(np.float32)[:, :, None] * theta).astype(np.float64)
    c[:, C_COS:C_SIN] = np.cos(angle).reshape(P, -1)
    c[:, C_SIN:C_END] = np.sin(angle).reshape(P, -1)
    return c


TIMETABLE = {
    "PE": {
        "norm1": [(-489116, -470709, -313685, -316205, -311830)],
        "gate1": [(-471062, -332577, -312166, -302423, -310155)],
        "hid1": [(-465571, -280474, -296810, -290108, -297343)],
        "normm": [(-407612, -280087, -277969, -277025, -275277)],
        "proj": [(-393684, -274859, -268733, -267659, -263086)],
        "index0": [(-382944, -274790, -253013, -261927, -249331)],
        "index1": [(-341812, -269892, -248075, -251857, -241995)],
        "index2": [(-328266, -259071, -244170, -246469, -238066)],
        "index3": [(-283304, -232428, -236939, -240985, -233178)],
        "query": [(-266896, -222631, -222764, -231378, -233052)],
        "keysT": [(-203211, -214660, -221211, -223212, -206055)],
        "cwin": [(-194322, -209435, -211310, -202057, -162914)],
        "queryT0": [(-193312, -208542, -198435, -194300, -152006)],
        "queryT1": [(-180223, -195419, -188451, -185786, -98744)],
        "key": [(-146315, -72882, -46162, -58775, -60818), (-107512, -30887, -32391, -40396, -37591),
                (-68190, -22472, 2118, -32132, -10845), (-6774, 21320, 22040, 16943, 34243)],
        "score": [(-101250, -29998, -31084, -34788, -24589), (-17392, -10183, -497, 3635, -3994),
                  (12501, 21338, 20629, 32514, 13976), (32283, 54183, 44576, 57178, 89975)],
        "turn": [(-8852, -8497, -1791, 13027, -12156), (11013, 35193, 28852, 36654, 7242),
                 (35061, 41676, 49531, 58847, 101937), (83695, 75333, 69218, 78492, 121735)],
        "value": [(-1110, 19898, 2390, 31254, 4329), (25070, 40580, 36329, 54258, 39008),
                  (58240, 58531, 60288, 62624, 114850), (89449, 81795, 83832, 83020, 184359)],
        "mix": [(123339, 119899, 111705, 96683, 236529)],
        "norm2": [(150040, 136367, 136125, 150068, 244098)],
        "gate2": [(153196, 140480, 137586, 199468, 291449)],
        "hid2": [(176830, 173515, 181662, 256803, 310744)],
    },
    "ACT": {
        "stat1": [(-452063, -454677, -323109, -342336, -337127)],
        "norm1": [(-441588, -365033, -307993, -309417, -313047)],
        "gate1": [(-388626, -332667, -296691, -300251, -300431)],
        "act1": [(-379746, -329045, -290395, -297531, -294505)],
        "sum1": [(-323067, -315247, -274397, -280615, -275427)],
        "normm": [(-323040, -289099, -269519, -268034, -272412)],
        "proj": [(-313146, -282851, -256774, -260355, -259925)],
        "krow": [(-297299, -276798, -252275, -254183, -251903)],
        "index0": [(-267094, -267499, -249875, -249669, -246393)],
        "index1": [(-258822, -231427, -244008, -248216, -245428)],
        "index2": [(-246032, -231100, -240827, -244384, -235688)],
        "index3": [(-243924, -229443, -236522, -233736, -231224)],
        "query": [(-239440, -214234, -211855, -229469, -198874)],
        "keysT": [(-230439, -206140, -201852, -203633, -174143)],
        "cwin": [(-222093, -183720, -190148, -180977, -149296)],
        "queryT0": [(-217489, -179332, -184589, -175005, -97399)],
        "queryT1": [(-204245, -172398, -171779, -172450, -83698)],
        "key": [(-104904, -41508, -41088, -50769, -52229), (-94658, -18742, -21844, -27250, -21132),
                (-46725, 20348, 15210, 27054, 15875), (16725, 32852, 43993, 34955, 77052)],
        "score": [(-16859, -12512, -16100, -9524, 993), (9534, 23894, 14164, 28092, 24995),
                  (38974, 31738, 36020, 37973, 71065), (78440, 60010, 61511, 54414, 111231)],
        "weigh": [(-1725, 5953, -3400, 7993, 1081), (13565, 30890, 22919, 35417, 32695),
                  (39812, 43033, 45276, 42160, 110848), (84957, 78939, 69912, 72044, 216990)],
        "turn": [(8813, 13652, 8114, 28765, 15352), (27692, 33438, 32454, 37771, 57966),
                 (44088, 49704, 52699, 49744, 125374), (98982, 82185, 78608, 81234, 225567)],
        "mix": [(144673, 131501, 131897, 135990, 286888)],
        "norm2": [(154461, 136954, 136067, 200516, 296739)],
        "gate2": [(156161, 150085, 147071, 214190, 326632)],
        "act2": [(169674, 155393, 165307, 288123, 329855)],
    },
    "DVE": {
        "stat1": [(-442858, -487541, -387083, -384753, -378771)],
        "norm1": [(-429055, -468289, -349531, -348502, -341521)],
        "act1": [(-415745, -377458, -335491, -332886, -338937)],
        "hid1": [(-405272, -377329, -328047, -328871, -334401)],
        "sum1": [(-396488, -361483, -325295, -325238, -328936)],
        "normm": [(-380409, -345870, -320849, -319978, -319870)],
        "krow": [(-331079, -296710, -293355, -299338, -293830)],
        "index0": [(-328772, -287618, -283860, -284772, -282783)],
        "index1": [(-318141, -285370, -281382, -283767, -276855)],
        "index2": [(-300504, -273032, -277229, -270512, -274158)],
        "index3": [(-299057, -253471, -273110, -262090, -271135)],
        "pick0": [(-226929, -251927, -257673, -257893, -260993)],
        "rope0": [(-297487, -242822, -236351, -230289, -228261)],
        "rope1": [(-265310, -239092, -227390, -220163, -169549)],
        "pick1": [(-212425, -246854, -243837, -240069, -249793)],
        "key": [(-225971, -132945, -116183, -108696, -104102), (-179153, -93807, -109256, -86971, -86991),
                (-114804, -81668, -82433, -78034, -42569), (-46495, -29727, -23566, -61764, 24458)],
        "pick2": [(-200102, -233002, -209699, -208653, -235648)],
        "pick3": [(-196171, -225804, -198400, -196700, -198385)],
        "score": [(-58184, -59042, -58587, -63574, -57520), (-37539, -27194, -31285, -20322, -36851),
                  (-15995, -15477, -14344, -2060, 41246), (7178, 18738, 6655, 13701, 103433)],
        "turn": [(-41957, -44307, -45073, -58988, -53014), (-29700, -19302, -25582, -7695, -36021),
                 (-5529, -8902, -6146, 4714, 85067), (35782, 27533, 25376, 19330, 134292)],
        "value": [(-29074, -21342, -26890, -10752, 9332), (-411, 10994, -5387, 12249, 75458),
                  (19691, 25513, 22417, 20052, 200590), (66280, 63622, 60467, 60761, 229959)],
        "mix": [(97361, 83890, 84700, 73034, 240681)],
        "norm2": [(112666, 87902, 87228, 168219, 242988)],
        "act2": [(120321, 114363, 115339, 218199, 315286)],
        "hid2": [(135120, 123767, 127789, 242243, 334819)],
        "sum2": [(149192, 144687, 146882, 313066, 348152)],
    },
    "SP": {
        "krow": [(-200000,) * 5],
        "store": [(110000,) * 5],
    },
}
AHEAD1, BEHIND = 3, -1
BY_DUO = ("key", "weigh", "score", "turn", "value")


def stage(n):
    return n if n < 2 else 2 if n < TILES - 2 else n - TILES + 5


def run_parts(engine, parts, setup=()):
    setup = dict(setup)
    places = []
    for part in parts:
        for d, times in enumerate(TIMETABLE[engine][part]):
            places += [(n + times[stage(n)] / 100000, part, n, d) for n in range(TILES)]
    for _, part, n, d in sorted(places):
        if part in BY_DUO:
            parts[part](n, d)
        else:
            parts[part](n)
            if n == 0 and part in setup:
                setup[part]()


def columns(n):
    i = n % TPB
    return TOPK if i == 0 else P * i + LW


def known(n, d):
    return n % TPB == 0 and (d + 1) * DUO <= LW


def slot(g):
    d, q, k = g // (2 * GROUP), g // GROUP % 2, g % GROUP
    return 2 * GROUP * d + 2 * k + q


def chunks(n):
    w = columns(n)
    return [(a, min(512, w - a)) for a in range(0, w, 512)]


def fills(n):
    return NI * len(chunks(n))


def fills_before(n):
    return sum(fills(m) for m in range(n))


def quarter(n, j):
    all_fills = [(h, a, w) for a, w in chunks(n) for h in range(NI)]
    k = len(all_fills) // 4
    return [(fills_before(n) + f, *all_fills[f]) for f in range(j * k, (j + 1) * k)]


def macaron_block(nc, x, w_dkv, w_uk, w_uv, w_dq, w_uq, w_qr, w_kr, w_out, iwq, iwk, iw, raw_delta,
                  w_gate, w_up, w_down, consts, out):
    with ExitStack() as ctx:
        def sb(name, shape, dt=F32):
            return ctx.enter_context(nc.sbuf_tensor(name, shape, dt))

        def bank(name):
            return ctx.enter_context(nc.psum_tensor(name, [P, 512], F32))

        def sem(name):
            return ctx.enter_context(nc.semaphore(name))

        table = nc.dram_tensor("key_table", [BATCH * LEN, KD], F32).ap()

        ps_f1, ps_f2, ps_i0, ps_i1, ps_tk, ps_tp = [
            bank(m) for m in ("ps_f1", "ps_f2", "ps_i0", "ps_i1", "ps_tk", "ps_tp")]
        ps_i = (ps_i0, ps_i1)
        ps_ss = ctx.enter_context(nc.psum_tensor("ps_ss", [P, 2, 512], F32))
        ps_s = (ps_ss[:, 0, :], ps_ss[:, 1, :])
        ps_s0, ps_s1 = ps_s
        ps_ckr = ps_i0[:, P:P + KD]

        def turned_in(k):
            return ps_i0[:, 0:P] if k == "m" else ps_f1[:, HID:512]

        cst = sb("cst", [P, C_END])
        ident = cst[:, C_ID:C_ID + P]
        wg_i = sb("wg_i", [P, HC, D], I32)
        wu_i = sb("wu_i", [P, HC, D], I32)
        wd_i = sb("wd_i", [P, HC, P], I32)
        wg_f = sb("wg_f", [P, HC, D])
        wu_f = sb("wu_f", [P, HC, D])
        wd_f = sb("wd_f", [P, HC, P])
        wgT = sb("wgT", [P, HC, P])
        wuT = sb("wuT", [P, HC, P])
        wdT = sb("wdT", [P, HC, D])
        wckr = sb("wckr", [P, KD])
        wiq = sb("wiq", [P, NI * DH])
        wik = sb("wik", [P, 2 * DH])
        iw_b = sb("iw_b", [P, NI])
        wuq_s = sb("wuq_s", [DQ, NH * DH])
        wuk_s = sb("wuk_s", [DC, NH * DH])
        wuv_s = sb("wuv_s", [DC, NH * DH])
        wdq_s = sb("wdq_s", [P, DQ])
        wout_s = sb("wout_s", [P, NH // 2, D])
        up_T = sb("up_T", [P, NH // 2, DQ + 2 * DC])
        wdqT = sb("wdqT", [DQ, P])
        wq64 = sb("wq64", [DQ, NH, KD])
        wqf = sb("wqf", [P, NH * KD])
        wvo = sb("wvo", [P, NH, D])
        delta = sb("delta", [P, 8, HALF])
        trig = sb("trig", [P, NTRIG, 4, HALF])
        trt = sb("trt", [P, 2, NTRIG, HALF])

        xs = sb("xs", [P, TILES, D])
        stats = {k: sb("stats" + k, [P, 6]) for k in "1m2"}
        mv = {k: sb("mv" + k, [P, 2]) for k in "1m2"}
        rstd = {k: sb("rstd" + k, [P, 1]) for k in "1m2"}
        rln = {k: sb("rln" + k, [P, 1]) for k in "1m2"}
        eps = sb("eps", [P, 1])
        xn = {k: sb("xn" + k, [P, D]) for k in "1m2"}
        xnT = {k: sb("xnT" + k, [P, P]) for k in "1m2"}
        x1nT = xnT["m"]
        f_abs = sb("f_abs", [P, HID])
        f_ln = sb("f_ln", [P, HID])
        f_sig = sb("f_sig", [P, HID])
        f_gu = sb("f_gu", [P, HID])
        hid = sb("hid", [P, HC, P])

        qiT = sb("qiT", [P, NI, P])
        kiT = sb("kiT", [P, BATCH, LEN])
        pos_s = sb("pos_s", [P, NI, ICOLS])
        isc = sb("isc", [P, ICOLS])
        top8 = sb("top8", [P, SEL])
        idx = sb("idx", [P, SEL], U32)
        idxT = sb("idxT", [P, RING, NG], U32)

        k_abs = sb("k_abs", [P, DR])
        k_ln = sb("k_ln", [P, DR])
        rows = sb("rows", [P, RING, KD + DR])
        k_rot = sb("k_rot", [P, 2 * DR])
        krow = sb("krow", [P, 2, KD])
        keysT = sb("keysT", [P, RING, LW + P])
        c_win = sb("c_win", [WIN, RING, P // QUAD, DC])
        gath = sb("gath", [P, RING, NG, KD])
        g_rot = sb("g_rot", [P, 2 * GROUP, 2 * DR])

        q_abs = sb("q_abs", [P, NH, DR])
        q_ln = sb("q_ln", [P, NH, DR])
        q_mu = sb("q_mu", [P, NH, 2 * DR])
        q_rot = sb("q_rot", [P, NH, 2 * DR])
        qrow = sb("qrow", [P, 2, NH, KD])
        qT = sb("qT", [P, RING, 2, ND, QUAD, NH])

        kT = sb("kT", [P, 2, 512])
        sm = sb("sm", [P, 2, SW])
        nmx = sb("nmx", [P, 2])
        den = sb("den", [P, 2])
        rden = sb("rden", [P, 2])
        pr = sb("pr", [P, 2, 2, SW])
        prT = sb("prT", [P, 2, 2, SC // NH, NH])
        prTw = sb("prTw", [WIN, 2, 2, QUAD, NH])
        oT = sb("oT", [P, 2, P, NH])

        x_in = [sem("x_first_in"), sem("x_rest_in")]
        ffn_w_in = [sem("w_gate_in"), sem("w_up_in"), sem("w_down_in")]
        delta_in, ident_in = sem("delta_in"), sem("ident_in")
        cst_in, proj_w_in, lat_w_in, out_done = sem("cst_in"), sem("proj_w_in"), sem("lat_w_in"), sem("out_done")
        known_in = sem("known_rows_in")
        table_in = [sem(f"table_in{r}") for r in range(RING)]
        gathered = [[sem(f"gathered{r}_{d}") for d in range(ND)] for r in range(RING)]
        R = {m: sem(m) for m in (
            "wf", "eps", "rl1", "rlm", "rl2", "w_T", "w_Ts", "trig_e", "trig_s", "trig_a", "trig_sin", "trig_done",
            "lat_T", "lat_Ts", "lat_w", "lat_ws", "wqf_p", "wqf_s",
            "x1_down", "x1", "x2_y", "x2", "x3_down", "x3",
            "st1", "mv1", "rs1", "xn1", "xT1", "xTs1", "stm", "mvm", "rsm", "xnm", "xTm", "xTsm",
            "st2", "mv2", "rs2", "xn2", "xT2", "xTs2",
            "gu1", "ab1", "ex1", "ln1", "lsig1", "sig1", "gu_s1", "hid1",
            "gu2", "ab2", "ex2", "ln2", "lsig2", "sig2", "gu_s2", "hid2",
            "proj", "qki", "k_ab", "k_ex", "k_lnd", "rows_c", "rows_mu", "rows_all", "krot_m", "krow_done",
            "iscore", "irelu", "isum", "top", "topi", "idx_T", "idx_done",
            "qproj", "q_ab", "q_ex", "q_lnd", "q_c", "q_mud", "q_rm", "qrow_done", "qT_p", "qT_done",
            "keysT_p", "keysT_done", "cwin_p", "cwin_done",
            "g_rm", "g_done", "kT_p", "kT_done", "score", "smax", "prob", "rdend", "prob_n",
            "prT_p", "prT_done", "value", "o_done")}

        block = ctx.enter_context(nc.Block())

        @block.sync
        def _(sp):
            sp.dma_start(xs[:, 0, :], x[0, 0:P, :]).then_inc(x_in[0], 16)
            sp.dma_start(wg_i[:, :, :], w_gate.rearrange("(c p) d -> p c d", p=P)).then_inc(ffn_w_in[0], 16)
            sp.dma_start(wd_i[:, :, :], w_down.rearrange("d (c p) -> d c p", p=P)).then_inc(ffn_w_in[2], 16)
            for src, dst in ((w_dkv, wckr[:, 0:DC]), (w_kr, wckr[:, DC:KD]), (iwq, wiq[:, :]),
                             (iwk, wik[:, 0:DH]), (iwk, wik[:, DH:2 * DH])):
                sp.dma_start(dst, src).then_inc(proj_w_in, 16)
            for b in range(BATCH):
                lo = 1 if b == 0 else 0
                sp.dma_start(xs[:, b * TPB + lo:(b + 1) * TPB, :],
                             x[b, lo * P:, :].rearrange("(t p) d -> p t d", p=P)).then_inc(x_in[1], 16)

            def table_rows(n):
                sp.wait_ge(R["rows_all"], 2 * (n + 1))
                sp.wait_ge(R["rows_mu"], n + 1)
                sp.wait_ge(R["rows_c"], 2 * n + 1)
                sp.dma_start(table[n * P:(n + 1) * P, :], rows[:, n % RING, 0:KD]).then_inc(table_in[n % RING], 16)
                if n % TPB == 0:
                    known_rows(n)

            def store(n):
                sp.wait_ge(R["x3"], n + 1)
                b, i = n // TPB, n % TPB
                sp.dma_start(out[b, i * P:(i + 1) * P, :], xs[:, n, :]).then_inc(out_done, 16)

            def known_rows(n):
                sp.wait_ge(table_in[n % RING], 16 * (n // RING + 1))
                if n:
                    sp.wait_ge(R["value"], ND * (n - RING) + ND)
                for j in range(GROUP):
                    rows_in = table[n * P + LW:n * P + TOPK, :].rearrange("(p a) k -> p a k", a=1)
                    sp.dma_start(gath[j * SEL:(j + 1) * SEL, n % RING, 0:LW // GROUP, :],
                                 rows_in.to_broadcast([SEL, LW // GROUP, KD])).then_inc(known_in, 16)

            run_parts("SP", {"krow": table_rows, "store": store})
            sp.wait_ge(out_done, 16 * TILES)

        @block.gpsimd
        def _(pool):
            for n in range(TILES):
                pool.wait_ge(R["idx_done"], n + 1)
                pool.wait_ge(table_in[n % RING], 16 * (n // RING + 1))
                for g in range(LW // GROUP if n % TPB == 0 else 0, NG):
                    pool.indirect_dma_start(
                        gath[:, n % RING, slot(g), :], None, table[0:(n + 1) * P, :],
                        bass.IndirectOffsetOnAxis(ap=idxT[:, n % RING, g:g + 1], axis=0),
                    ).then_inc(gathered[n % RING][g // (2 * GROUP)], 16)

        @block.scalar
        def _(act):
            act.dma_start(delta[:, 0, :], raw_delta.rearrange("(a d) -> a d", a=1).partition_broadcast(P)).then_inc(delta_in, 16)
            act.dma_start(wu_i[:, :, :], w_up.rearrange("(c p) d -> p c d", p=P)).then_inc(ffn_w_in[1], 16)
            act.dma_start(ident, consts[:, 0:P]).then_inc(ident_in, 16)
            act.dma_start(cst[:, P:C_END], consts[:, P:C_END]).then_inc(cst_in, 16)
            act.dma_start(iw_b[:, :], iw.rearrange("(a d) -> a d", a=1).partition_broadcast(P)).then_inc(cst_in, 16)
            for src, dst in ((w_uq, wuq_s[:, :]), (w_uk, wuk_s[:, :]), (w_uv, wuv_s[:, :]), (w_dq, wdq_s[:, :]),
                             (w_out.rearrange("(c p) d -> p c d", p=P), wout_s[:, :, :]),
                             (w_qr.rearrange("q (h r) -> q h r", r=DR), wq64[:, :, DC:KD])):
                act.dma_start(dst, src).then_inc(lat_w_in, 16)

            nc.scalar.preload_act_table_set("natural_log_exp_and_others")
            act.wait_ge(delta_in, 16)
            nc.scalar.activation(delta[:, 1, :], delta[:, 0, :], ACT.Exp, scale=-1.0).then_inc(R["trig_e"], 1)
            act.wait_ge(R["eps"], 1)
            act.wait_ge(R["w_T"], 3)
            nc.scalar.copy(wgT[:, :, :].rearrange("p a b -> p (a b)"), ps_f1[:, 0:HID])
            nc.scalar.copy(wuT[:, :, :].rearrange("p a b -> p (a b)"), ps_f2[:, 0:HID])
            nc.scalar.copy(wdT[:, :, :].rearrange("p a b -> p (a b)"), ps_i0[:, 0:HID]).then_inc(R["w_Ts"], 1)

            act.wait_ge(R["lat_T"], 1)
            nc.scalar.copy(up_T[:, :, :].rearrange("p a b -> p (a b)"), ps_s0[:, :])
            nc.scalar.copy(wdqT[:, :], ps_s1[0:DQ, 0:P]).then_inc(R["lat_Ts"], 1)

            def setup_sines():
                act.wait_ge(R["trig_a"], 1)
                nc.scalar.activation(delta[:, 5:7, :], delta[:, 3:5, :], ACT.Sin).then_inc(R["trig_sin"], 1)
                nc.scalar.preload_act_table_set("natural_log_exp_and_others")

            def setup_products():
                act.wait_ge(R["lat_w"], 1)
                act.wait_ge(lat_w_in, 96)
                for e in range(2):
                    q4 = (ps_tk, ps_tp)[e][0:DQ, 0:4 * DC].rearrange("p (h c) -> p h c", c=DC)
                    nc.scalar.copy(wq64[:, e::2, 0:DC], q4).then_inc(R["lat_ws"], 1)
                for e in range(2):
                    nc.scalar.copy(wvo[:, e::2, :], ps_s[e].rearrange("p (h d) -> p h d", d=D)).then_inc(R["lat_ws"], 1)
                act.wait_ge(R["lat_ws"], 4)
                nc.scalar.activation(ps_ss[:, :, OUT:OUT + P],
                                     cst[:, C_MS:C_MS + 2 * P].rearrange("p (q t) -> p q t", q=2), ACT.Copy, scale=0.0)

            def setup_query():
                act.wait_ge(R["wqf_p"], 1)
                nc.scalar.copy(wqf[:, :], ps_tk[:, :]).then_inc(R["wqf_s"], 1)

            def stat(k, n):
                act.wait_ge(R["mv" + k], n + 1)
                nc.scalar.activation(rln[k][:, :], mv[k][:, 1:2], ACT.Ln, bias=eps[:, 0:1]).then_inc(R["rl" + k], 1)
                act.wait_ge(R["rl" + k], n + 1)
                nc.scalar.activation(rstd[k][:, :], rln[k][:, :], ACT.Exp, scale=-0.5).then_inc(R["rs" + k], 1)

            def turned(k):
                def part(n):
                    act.wait_ge(R["xT" + k], n + 1)
                    nc.scalar.copy(xnT[k][:, :], turned_in(k)).then_inc(R["xTs" + k], 1)
                return part

            def gate(k):
                def part(n):
                    act.wait_ge(R["gu" + k], n + 1)
                    nc.scalar.activation(f_abs[:, :], ps_f1[:, 0:HID], ACT.Abs).then_inc(R["ab" + k], 1)
                    act.wait_ge(R["ab" + k], n + 1)
                    nc.scalar.activation(f_abs[:, :], f_abs[:, :], ACT.Exp, scale=-1.0).then_inc(R["ex" + k], 1)
                    act.wait_ge(R["ex" + k], n + 1)
                    nc.scalar.activation(f_ln[:, :], f_abs[:, :], ACT.Ln, bias=1.0).then_inc(R["ln" + k], 1)
                return part

            def sigmoid(k):
                def part(n):
                    act.wait_ge(R["lsig" + k], n + 1)
                    nc.scalar.activation(f_sig[:, :], f_sig[:, :], ACT.Exp).then_inc(R["sig" + k], 1)
                return part

            def proj(n):
                b, i, r = n // TPB, n % TPB, n % RING
                act.wait_ge(R["proj"], n + 1)
                if n == 0:
                    act.wait_ge(R["eps"], 2)
                for e in range(2):
                    half = slice(e * DH, (e + 1) * DH)
                    nc.scalar.copy(qiT[half, e::2, :].rearrange("p c (j g) -> p c g j", j=GROUP),
                                   ps_i1[half, 0:2 * P].rearrange("p (c g j) -> p c g j", c=2, j=GROUP))
                nc.scalar.copy(kiT[:, b, i * P:(i + 1) * P], ps_i1[:, 2 * P:3 * P]).then_inc(R["qki"], 1)
                nc.scalar.activation(k_abs[:, :], ps_ckr[:, DC:KD], ACT.Abs).then_inc(R["k_ab"], 1)
                nc.scalar.copy(rows[:, r, 0:DC], ps_ckr[:, 0:DC]).then_inc(R["rows_c"], 1)
                act.wait_ge(R["k_ab"], n + 1)
                nc.scalar.activation(k_abs[:, :], k_abs[:, :], ACT.Exp, scale=-1.0).then_inc(R["k_ex"], 1)
                act.wait_ge(R["k_ex"], n + 1)
                nc.scalar.activation(k_ln[:, :], k_abs[:, :], ACT.Ln, bias=1.0).then_inc(R["k_lnd"], 1)

            def index(j):
                def part(n):
                    for f, h, a, w in quarter(n, j):
                        act.wait_ge(R["iscore"], f + 1)
                        nc.scalar.activation(pos_s[:, h, a:a + w], ps_i[1 - h % 2][:, 0:w], ACT.Relu).then_inc(R["irelu"], 1)
                return part

            def krow_c(n):
                src = rows[:, n % RING, 0:DC]
                act.wait_ge(R["rows_c"], 2 * n + 1)
                nc.scalar.copy(krow[:, 0, 0:DC], src)
                nc.scalar.copy(krow[:, 1, 0:DC], src).then_inc(R["rows_c"], 1)

            def query(n):
                act.wait_ge(R["qproj"], n + 1)
                q = ps_i0[:, :].rearrange("p (h k) -> p h k", k=KD)
                nc.scalar.activation(q_abs[:, :, :], q[:, :, DC:KD], ACT.Abs).then_inc(R["q_ab"], 1)
                nc.scalar.copy(qrow[:, 0, :, 0:DC], q[:, :, 0:DC])
                act.wait_ge(R["q_ab"], n + 1)
                nc.scalar.activation(q_abs[:, :, :], q_abs[:, :, :], ACT.Exp, scale=-1.0).then_inc(R["q_ex"], 1)
                nc.scalar.copy(qrow[:, 1, :, 0:DC], q[:, :, 0:DC]).then_inc(R["q_c"], 1)
                act.wait_ge(R["q_ex"], n + 1)
                nc.scalar.activation(q_ln[:, :, :], q_abs[:, :, :], ACT.Ln, bias=1.0).then_inc(R["q_lnd"], 1)

            def keys_turned(n):
                act.wait_ge(R["keysT_p"], n + 1)
                if n % TPB < TPB - 1:
                    nc.scalar.copy(keysT[:, (n + 1) % RING, 0:LW], ps_i1[:, P - LW:P])
                nc.scalar.copy(keysT[:, n % RING, LW:LW + P], ps_i1[:, 0:P]).then_inc(R["keysT_done"], 1)

            def queryT(v):
                def part(n):
                    r = n % RING
                    act.wait_ge(R["qT_p"], 2 * n + v + 1)
                    for e in range(2):
                        src = ps_i[v][e * KD:(e + 1) * KD, :].rearrange("k (h d q t) -> k q d h t", h=NH // 2, q=2, t=QUAD)
                        for par in range(2):
                            for d in range(ND):
                                dst = qT[par * KD:(par + 1) * KD, r, v, d, :, e::2].rearrange("k t h -> k h t")
                                last = nc.scalar.copy(dst, src[:, par, d])
                    last.then_inc(R["qT_done"], 1)
                return part

            def cwin(n):
                act.wait_ge(R["cwin_p"], n + 1)
                nc.scalar.copy(c_win[:, n % RING, :, :].rearrange("p q c -> p (q c)"),
                               ps_i1[0:WIN, P:P + (P // QUAD) * DC]).then_inc(R["cwin_done"], 1)

            def key(n, d):
                k = n * ND + d
                act.wait_ge(R["kT_p"], k + 1)
                nc.scalar.copy(kT[:, k % 2, :], ps_tk[:, :]).then_inc(R["kT_done"], 1)

            def score(n, d):
                k = n * ND + d
                act.wait_ge(R["smax"], k + 1)
                for q in range(2):
                    last = nc.scalar.activation(pr[:, k % 2, q, :], sm[:, q, :], ACT.Exp, bias=nmx[:, q:q + 1],
                                                scale=-1.0, accum_out=den[:, q:q + 1])
                last.then_inc(R["prob"], 1)

            def weigh(n, d):
                k = n * ND + d
                act.wait_ge(R["rdend"], k + 1)
                for q in range(2):
                    last = nc.scalar.activation(pr[:, k % 2, q, :], pr[:, k % 2, q, :], ACT.Copy, scale=rden[:, q:q + 1])
                last.then_inc(R["prob_n"], 1)

            def turn(n, d):
                k = n * ND + d
                act.wait_ge(R["prT_p"], k + 1)
                nc.scalar.copy(prT[:, k % 2].rearrange("p q t h -> p (q t h)"), ps_tp[:, 0:2 * SC])
                nc.scalar.copy(prTw[:, k % 2].rearrange("p q t h -> p (q t h)"),
                               ps_tp[0:WIN, 2 * SC:512]).then_inc(R["prT_done"], 1)

            run_parts("ACT", {"stat1": lambda n: stat("1", n), "norm1": turned("1"), "gate1": gate("1"), "act1": sigmoid("1"),
                       "sum1": lambda n: stat("m", n), "normm": turned("m"), "proj": proj,
                       **{f"index{j}": index(j) for j in range(4)},
                       "krow": krow_c, "query": query, "keysT": keys_turned, "cwin": cwin, "queryT0": queryT(0), "queryT1": queryT(1),
                       "key": key, "score": score, "weigh": weigh, "turn": turn, "mix": lambda n: stat("2", n),
                       "norm2": turned("2"), "gate2": gate("2"), "act2": sigmoid("2")},
                      {"norm1": setup_sines, "act1": setup_products, "index3": setup_query})

        @block.vector
        def _(dve):
            nc.vector.memset(eps[:, :], EPS).then_inc(R["eps"], 1)
            nc.vector.memset(qiT[:, :, :], 0.0).then_inc(R["eps"], 1)
            for k, (src, dst) in enumerate(((wg_i, wg_f), (wu_i, wu_f), (wd_i, wd_f))):
                dve.wait_ge(ffn_w_in[k], 16)
                nc.vector.tensor_scalar(dst[:, :, :], src[:, :, :], WSCALE, None, ALU.mult).then_inc(R["wf"], 1)
            pi = float(np.pi)
            top = 3.1415925
            dve.wait_ge(R["trig_e"], 1)
            nc.vector.tensor_scalar(delta[:, 2, :], delta[:, 1, :], 1.0, None, ALU.add).then_inc(R["trig_s"], 1)
            dve.wait_ge(R["trig_s"], 1)
            nc.vector.reciprocal(delta[:, 2, :], delta[:, 2, :]).then_inc(R["trig_s"], 1)
            dve.wait_ge(R["trig_s"], 2)
            nc.vector.tensor_scalar(delta[:, 3, :], delta[:, 2, :], pi, None, ALU.mult)
            nc.vector.tensor_scalar(delta[:, 4, :], delta[:, 2, :], -2.0 * pi, pi, ALU.mult, ALU.add).then_inc(R["trig_s"], 1)
            dve.wait_ge(R["trig_s"], 3)
            nc.vector.tensor_scalar(delta[:, 3:5, :], delta[:, 3:5, :], top, -top, ALU.min, ALU.max).then_inc(R["trig_a"], 1)

            def trig_tables():
                done = 0
                cd, sd = delta[:, 7:8, :], delta[:, 6:7, :]
                dve.wait_ge(R["trig_sin"], 1)
                nc.vector.tensor_tensor(delta[:, 7, :], delta[:, 5, :], delta[:, 5, :], ALU.mult).then_inc(R["trig_s"], 1)
                dve.wait_ge(R["trig_s"], 4)
                nc.vector.tensor_scalar(delta[:, 7, :], delta[:, 7, :], -2.0, 1.0, ALU.mult, ALU.add).then_inc(R["trig_s"], 1)
                dve.wait_ge(R["trig_s"], 5)
                dve.wait_ge(cst_in, 32)
                cb = cst[:, C_COS:C_SIN].rearrange("p (n f) -> p n f", f=HALF)
                sn = cst[:, C_SIN:C_END].rearrange("p (n f) -> p n f", f=HALF)
                full = [P, NTRIG, HALF]
                for j, (u, v, op) in enumerate(((cb, sn, ALU.add), (sn, cb, ALU.subtract))):
                    nc.vector.tensor_tensor(trt[:, 0, :, :], u, cd.to_broadcast(full), ALU.mult)
                    nc.vector.tensor_tensor(trt[:, 1, :, :], v, sd.to_broadcast(full), ALU.mult).then_inc(R["trig_s"], 1)
                    dve.wait_ge(R["trig_s"], 6 + 2 * j)
                    dst = trig[:, :, 0, :] if j == 0 else trig[:, :, 3, :]
                    nc.vector.tensor_tensor(dst, trt[:, 0, :, :], trt[:, 1, :, :], op).then_inc(R["trig_s"], 1)
                    dve.wait_ge(R["trig_s"], 7 + 2 * j)
                nc.vector.tensor_copy(trig[:, :, 1, :], trig[:, :, 0, :])
                nc.vector.tensor_scalar(trig[:, :, 2, :], trig[:, :, 3, :], -1.0, None, ALU.mult).then_inc(R["trig_done"], 1)
                dve.wait_ge(R["trig_done"], 1)

            def stat(k, n):
                nc.vector.bn_stats(stats[k][:, :], xs[:, n, :]).then_inc(R["st" + k], 1)
                dve.wait_ge(R["st" + k], n + 1)
                nc.vector.bn_aggr(mv[k][:, :], stats[k][:, :]).then_inc(R["mv" + k], 1)

            def normed(k):
                def part(n):
                    dve.wait_ge(R["rs" + k], n + 1)
                    nc.vector.tensor_scalar(xn[k][:, :], xs[:, n, :], mv[k][:, 0:1], rstd[k][:, 0:1], ALU.subtract,
                                            ALU.mult).then_inc(R["xn" + k], 1)
                    if k == "m" and n == 0:
                        trig_tables()
                return part

            def stat1(n):
                dve.wait_ge(x_in[min(n, 1)], 16 if n == 0 else 32)
                stat("1", n)

            def log_sigmoid(k):
                def part(n):
                    dve.wait_ge(R["ln" + k], n + 1)
                    nc.vector.scalar_tensor_tensor(f_sig[:, :], ps_f1[:, 0:HID], 0.0, f_ln[:, :],
                                                   ALU.min, ALU.subtract).then_inc(R["lsig" + k], 1)
                return part

            def hidden(k):
                def part(n):
                    dve.wait_ge(R["sig" + k], n + 1)
                    nc.vector.tensor_tensor(f_gu[:, :], ps_f1[:, 0:HID], f_sig[:, :], ALU.mult).then_inc(R["gu_s" + k], 1)
                    dve.wait_ge(R["gu_s" + k], n + 1)
                    nc.vector.tensor_tensor(hid[:, :, :].rearrange("p a b -> p (a b)"), ps_f2[:, 0:HID], f_gu[:, :],
                                            ALU.mult).then_inc(R["hid" + k], 1)
                return part

            def sum1(n):
                dve.wait_ge(R["x1_down"], n + 1)
                nc.vector.scalar_tensor_tensor(xs[:, n, :], ps_f2[:, HID:512], 0.5, xs[:, n, :],
                                               ALU.mult, ALU.add).then_inc(R["x1"], 1)
                dve.wait_ge(R["x1"], n + 1)
                stat("m", n)

            def krow_rot(n):
                i, r = n % TPB, n % RING
                dve.wait_ge(R["k_lnd"], n + 1)
                for dst, a in ((DC, 0), (DC + DR, HALF), (DC + DR + HALF, 0)):
                    w = DR if dst == DC else HALF
                    ins = nc.vector.scalar_tensor_tensor(rows[:, r, dst:dst + w], ps_ckr[:, DC + a:DC + a + w], 0.0,
                                                         k_ln[:, a:a + w], ALU.max, ALU.add)
                    ins.then_inc(R["rows_mu"] if dst == DC else R["rows_all"], 1)
                dve.wait_ge(R["rows_all"], 2 * (n + 1))
                dve.wait_ge(R["rows_mu"], n + 1)
                nc.vector.tensor_tensor(k_rot[:, :], rows[:, r, DC:KD + DR], trig[:, i, :, :].rearrange("p a f -> p (a f)"),
                                        ALU.mult).then_inc(R["krot_m"], 1)
                dve.wait_ge(R["krot_m"], n + 1)
                for c in range(2):
                    nc.vector.tensor_tensor(krow[:, c, DC:KD], k_rot[:, 0:DR], k_rot[:, DR:2 * DR],
                                            ALU.add).then_inc(R["krow_done"], 1)

            def index(j):
                def part(n):
                    for f, h, a, w in quarter(n, j):
                        dve.wait_ge(R["irelu"], f + 1)
                        dst = isc[:, a:a + w]
                        if h == 0:
                            ins = nc.vector.tensor_scalar(dst, pos_s[:, 0, a:a + w], iw_b[:, 0:1], None, ALU.mult)
                        else:
                            dve.wait_ge(R["isum"], f + n)
                            ins = nc.vector.scalar_tensor_tensor(dst, pos_s[:, h, a:a + w], iw_b[:, h:h + 1], dst,
                                                                 ALU.mult, ALU.add)
                        ins.then_inc(R["isum"], 1)
                    if j == 3:
                        index_masks(n)
                return part

            def index_masks(n):
                i = n % TPB
                m = cst[:, C_M0:C_M0 + TOPK] if i == 0 else cst[:, C_M1:C_M1 + P]
                w = columns(n)
                dst = isc[:, w - m.shape[1]:w]
                s = fills_before(n + 1) + n
                dve.wait_ge(R["isum"], s)
                nc.vector.tensor_tensor(dst, dst, m, ALU.add).then_inc(R["isum"], 1)
                dve.wait_ge(R["isum"], s + 1)

            def pick(k):
                def part(n):
                    if n:
                        pick_eight(n, k)
                    elif k == 0:
                        for j in range(4):
                            pick_eight(0, j)
                return part

            def pick_eight(n, k):
                w, e = columns(n), slice(8 * k, 8 * k + 8)
                base = 7 * n + 2 * k
                nc.vector.max(top8[:, e], isc[:, 0:w]).then_inc(R["top"], 1)
                dve.wait_ge(R["top"], base + 1)
                nc.vector.max_index(idx[:, e], top8[:, e], isc[:, 0:w]).then_inc(R["topi"], 1)
                if k < 3:
                    nc.vector.match_replace(isc[:, 0:w], top8[:, e], isc[:, 0:w], TAKEN).then_inc(R["top"], 1)
                    dve.wait_ge(R["top"], base + 2)
                else:
                    dve.wait_ge(R["topi"], 4 * n + 4)
                    r = n % RING
                    if n < TPB:
                        nc.vector.transpose(idxT[:, r, :], idx[:, :]).then_inc(R["idx_done"], 1)
                    else:
                        nc.vector.transpose(idxT[:, r, :], idx[:, :]).then_inc(R["idx_T"], 1)
                        dve.wait_ge(R["idx_T"], n - TPB + 1)
                        nc.vector.tensor_scalar(idxT[:, r, :], idxT[:, r, :], float(LEN), None, ALU.add).then_inc(R["idx_done"], 1)

            def rope0(n):
                q = ps_i0[:, :].rearrange("p (h k) -> p h k", k=KD)
                dve.wait_ge(R["q_lnd"], n + 1)
                for dst, a in ((0, 0), (DR, HALF), (DR + HALF, 0)):
                    w = DR if dst == 0 else HALF
                    nc.vector.scalar_tensor_tensor(q_mu[:, :, dst:dst + w], q[:, :, DC + a:DC + a + w], 0.0,
                                                   q_ln[:, :, a:a + w], ALU.max, ALU.add).then_inc(R["q_mud"], 1)
                dve.wait_ge(R["q_mud"], 3 * (n + 1))
                rope(n, 0)

            def rope1(n):
                dve.wait_ge(R["qrow_done"], 2 * n + 1)
                rope(n, 1)

            def rope(n, v):
                i = n % TPB
                tr = trig[:, i + v * TPB, :, :].rearrange("p (o a) f -> p o (a f)", o=1).to_broadcast([P, NH, 2 * DR])
                nc.vector.tensor_tensor(q_rot[:, :, :], q_mu[:, :, :], tr, ALU.mult).then_inc(R["q_rm"], 1)
                dve.wait_ge(R["q_rm"], 2 * n + v + 1)
                nc.vector.tensor_tensor(qrow[:, v, :, DC:KD], q_rot[:, :, 0:DR], q_rot[:, :, DR:2 * DR],
                                        ALU.add).then_inc(R["qrow_done"], 1)

            def key(n, d):
                r, k = n % RING, n * ND + d
                if known(n, d):
                    dve.wait_ge(known_in, 16 * GROUP * (n // TPB + 1))
                else:
                    times = sum(1 for m in range(r, n + 1, RING) if not known(m, d))
                    dve.wait_ge(gathered[r][d], 16 * 2 * GROUP * times)
                gs = slice(2 * GROUP * d, 2 * GROUP * (d + 1))
                tr = trig[:, RANKS, :, :].rearrange("p (o a) f -> p o (a f)", o=1).to_broadcast([P, 2 * GROUP, 2 * DR])
                mu = gath[:, r, gs, DC:KD]
                if k:
                    dve.wait_ge(R["g_done"], k)
                nc.vector.tensor_tensor(g_rot[:, :, 0:DR], mu, tr[:, :, 0:DR], ALU.mult)
                nc.vector.tensor_tensor(g_rot[:, :, DR:DR + HALF], mu[:, :, HALF:DR], tr[:, :, DR:DR + HALF], ALU.mult)
                nc.vector.tensor_tensor(g_rot[:, :, DR + HALF:2 * DR], mu[:, :, 0:HALF], tr[:, :, DR + HALF:2 * DR],
                                        ALU.mult).then_inc(R["g_rm"], 1)
                dve.wait_ge(R["g_rm"], k + 1)
                nc.vector.tensor_tensor(gath[:, r, gs, DC:KD], g_rot[:, :, 0:DR], g_rot[:, :, DR:2 * DR],
                                        ALU.add).then_inc(R["g_done"], 1)

            def score(n, d):
                k = n * ND + d
                dve.wait_ge(R["score"], k + 1)
                for q in range(2):
                    first = n % TPB == 0 and 2 * d + q < LW // QUAD
                    m = cst[:, C_MS0:C_MS0 + SW] if first else cst[:, C_MS:C_MS + SW]
                    last = nc.vector.tensor_tensor_reduce(sm[:, q, :], ps_s[q][:, 0:SW], m, -SCALE, 3.0e38, ALU.add,
                                                          ALU.min, nmx[:, q:q + 1])
                last.then_inc(R["smax"], 1)

            def turn(n, d):
                k = n * ND + d
                dve.wait_ge(R["prob"], k + 1)
                nc.vector.reciprocal(rden[:, :], den[:, :]).then_inc(R["rdend"], 1)

            def value(n, d):
                k = n * ND + d
                dve.wait_ge(R["value"], k + 1)
                nc.vector.tensor_copy(oT[:, n % 2, d * DUO:(d + 1) * DUO, :].rearrange("c (q t) h -> c q (t h)", q=2),
                                      ps_ss[:, :, OUT:OUT + P]).then_inc(R["o_done"], 1)

            def mix(n):
                dve.wait_ge(R["x2_y"], n + 1)
                nc.vector.tensor_tensor(xs[:, n, :], ps_f2[:, HID:512], xs[:, n, :], ALU.add).then_inc(R["x2"], 1)
                dve.wait_ge(R["x2"], n + 1)
                stat("2", n)

            def sum2(n):
                dve.wait_ge(R["x3_down"], n + 1)
                nc.vector.scalar_tensor_tensor(xs[:, n, :], ps_f2[:, HID:512], 0.5, xs[:, n, :],
                                               ALU.mult, ALU.add).then_inc(R["x3"], 1)

            run_parts("DVE", {"stat1": stat1, "norm1": normed("1"), "act1": log_sigmoid("1"), "hid1": hidden("1"),
                       "sum1": sum1, "normm": normed("m"), "krow": krow_rot,
                       **{f"index{j}": index(j) for j in range(4)}, "pick0": pick(0), "pick1": pick(1),
                       "pick2": pick(2), "pick3": pick(3), "rope0": rope0, "rope1": rope1, "key": key, "score": score, "turn": turn,
                       "value": value, "mix": mix, "norm2": normed("2"), "act2": log_sigmoid("2"), "hid2": hidden("2"),
                       "sum2": sum2})

        @block.tensor
        def _(pe):
            pe.wait_ge(ident_in, 16)
            for k, (src, dst) in enumerate(((wg_f, ps_f1), (wu_f, ps_f2), (wd_f, ps_i0))):
                pe.wait_ge(R["wf"], k + 1)
                for c in range(HC):
                    last = nc.tensor.transpose(dst[:, c * P:(c + 1) * P], src[:, c, :], ident)
                last.then_inc(R["w_T"], 1)

            pe.wait_ge(lat_w_in, 96)
            for c in range(NH // 2):
                cols = slice(c * P, (c + 1) * P)
                nc.tensor.transpose(ps_s0[:, c * P:c * P + DQ], wuq_s[:, cols], ident[0:DQ, 0:DQ])
                nc.tensor.transpose(ps_s0[:, c * P + DQ:c * P + DQ + DC], wuk_s[:, cols], ident[0:DC, 0:DC])
                nc.tensor.transpose(ps_s0[:, c * P + DQ + DC:(c + 1) * P], wuv_s[:, cols], ident[0:DC, 0:DC])
            nc.tensor.transpose(ps_s1[0:DQ, 0:P], wdq_s[:, :], ident).then_inc(R["lat_T"], 1)

            def setup_products():
                pe.wait_ge(R["lat_Ts"], 1)
                for h in range(NH):
                    e, c = h % 2, h // 2
                    rows_h = slice(e * DH, (e + 1) * DH)
                    nc.tensor.matmul((ps_tk, ps_tp)[e][0:DQ, c * DC:(c + 1) * DC], up_T[rows_h, c, 0:DQ],
                                     up_T[rows_h, c, DQ:DQ + DC], start=True, stop=True)
                    for j in range(GROUP):
                        last = nc.tensor.matmul(ps_s[e][j * DC:(j + 1) * DC, c * D:(c + 1) * D],
                                                up_T[rows_h, c, DQ + DC:DQ + 2 * DC], wout_s[rows_h, c, :],
                                                start=True, stop=True)
                last.then_inc(R["lat_w"], 1)

            def setup_query():
                pe.wait_ge(R["lat_ws"], 4)
                nc.tensor.matmul(ps_tk[:, :], wdqT[:, :], wq64[:, :, :].rearrange("p h k -> p (h k)"),
                                 start=True, stop=True).then_inc(R["wqf_p"], 1)

            def turned(k):
                def part(n):
                    if n == 0 and k == "1":
                        pe.wait_ge(R["w_Ts"], 1)
                    if k == "m" and n:
                        pe.wait_ge(R["qT_done"], 2 * n - 1)
                    if k == "1" and n > AHEAD1 - BEHIND:
                        pe.wait_ge(R["gu_s2"], n - (AHEAD1 - BEHIND))
                    elif k == "1" and n:
                        pe.wait_ge(R["gu_s1"], n)
                    pe.wait_ge(R["xn" + k], n + 1)
                    nc.tensor.transpose(turned_in(k), xn[k][:, :], ident).then_inc(R["xT" + k], 1)
                return part

            def gate_up(k, n):
                if k == "1" and n > AHEAD1 - BEHIND:
                    pe.wait_ge(R["x3"], n - (AHEAD1 - BEHIND))
                elif k == "1" and n:
                    pe.wait_ge(R["x1"], n)
                pe.wait_ge(R["xTs" + k], n + 1)
                for w, dst in ((wgT, ps_f1), (wuT, ps_f2)):
                    for c in range(HC):
                        last = nc.tensor.matmul(dst[:, c * P:(c + 1) * P], w[:, c, :], xnT[k][:, :], start=True, stop=True)
                last.then_inc(R["gu" + k], 1)

            def down(k, n):
                pe.wait_ge(R["hid" + k], n + 1)
                for c in range(HC):
                    last = nc.tensor.matmul(ps_f2[:, HID:512], hid[:, c, :], wdT[:, c, :], start=(c == 0), stop=(c == HC - 1))
                last.then_inc(R["x1_down" if k == "1" else "x3_down"], 1)

            def proj(n):
                if n == 0:
                    pe.wait_ge(proj_w_in, 80)
                pe.wait_ge(R["xTsm"], n + 1)
                if n:
                    pe.wait_ge(R["qT_done"], 2 * n)
                for c in range(NI // 2):
                    nc.tensor.matmul(ps_i1[:, c * P:(c + 1) * P], wiq[:, c * P:(c + 1) * P], x1nT[:, :], start=True, stop=True)
                nc.tensor.matmul(ps_i1[:, 2 * P:3 * P], wik[:, :], x1nT[:, :], start=True, stop=True)
                nc.tensor.matmul(ps_ckr, x1nT[:, :], wckr[:, :], start=True, stop=True).then_inc(R["proj"], 1)

            def index(j):
                def part(n):
                    b = n // TPB
                    for f, h, a, w in quarter(n, j):
                        e = h % 2
                        if f - fills_before(n) >= 2:
                            pe.wait_ge(R["irelu"], f - 1)
                        elif h == 0:
                            pe.wait_ge(R["qki"], n + 1)
                        else:
                            pe.wait_ge(R["rows_all"], 2 * (n + 1))
                        nc.tensor.matmul(ps_i[1 - e][:, 0:w], qiT[:, h, :], kiT[:, b, a:a + w],
                                         start=True, stop=True).then_inc(R["iscore"], 1)
                return part

            def query(n):
                if n == 0:
                    pe.wait_ge(R["wqf_s"], 1)
                pe.wait_ge(R["irelu"], fills_before(n + 1))
                nc.tensor.matmul(ps_i0[:, :], x1nT[:, :], wqf[:, :], start=True, stop=True).then_inc(R["qproj"], 1)

            def keys_turned(n):
                pe.wait_ge(R["krow_done"], 2 * (n + 1))
                pe.wait_ge(R["rows_c"], 2 * (n + 1))
                nc.tensor.transpose(ps_i1[:, 0:P], krow[:, :, :].rearrange("p a b -> p (a b)"), ident).then_inc(R["keysT_p"], 1)

            def queryT(v):
                def part(n):
                    pe.wait_ge(R["q_c"], n + 1)
                    pe.wait_ge(R["qrow_done"], 2 * n + v + 1)
                    if v == 1:
                        pe.wait_ge(R["cwin_done"], n + 1)
                    for c in range(NH // 2):
                        last = nc.tensor.transpose(ps_i[v][:, c * P:(c + 1) * P],
                                                   qrow[:, v, 2 * c:2 * c + 2, :].rearrange("p a b -> p (a b)"), ident)
                    last.then_inc(R["qT_p"], 1)
                return part

            def cwin(n):
                r = n % RING
                pe.wait_ge(R["keysT_done"], n + 1)
                for q in range(P // QUAD):
                    a = window(n, q)
                    last = nc.tensor.transpose(ps_i1[0:WIN, P + q * DC:P + (q + 1) * DC], keysT[0:DC, r, a:a + WIN], ident[0:DC, 0:DC])
                last.then_inc(R["cwin_p"], 1)

            def window(n, q):
                return max(QUAD * q, LW) if n % TPB == 0 else QUAD * q

            def key(n, d):
                r, k = n % RING, n * ND + d
                pe.wait_ge(R["g_done"], k + 1)
                if k:
                    pe.wait_ge(R["kT_done"], k)
                for g in range(GROUP):
                    a = slot(2 * GROUP * d + g)
                    pair = gath[:, r, a:a + 2, :].rearrange("p a k -> p (a k)")
                    last = nc.tensor.transpose(ps_tk[:, g * P:(g + 1) * P], pair, ident)
                last.then_inc(R["kT_p"], 1)

            def score(n, d):
                r, k = n % RING, n * ND + d
                pe.wait_ge(R["kT_done"], k + 1)
                pe.wait_ge(R["qT_done"], 2 * (n + 1))
                if k > 1:
                    pe.wait_ge(R["o_done"], k - 1)
                if k:
                    pe.wait_ge(R["smax"], k)
                for q in range(2):
                    half = slice(q * KD, (q + 1) * KD)
                    a = window(n, 2 * d + q)
                    nc.tensor.matmul(ps_s[q][:, SC:SW], qT[half, r, 1, d, :, :].rearrange("k t h -> k (t h)"),
                                     keysT[half, r, a:a + WIN], start=True, stop=True)
                    for g in range(GROUP):
                        last = nc.tensor.matmul(
                            ps_s[q][g * SEL:(g + 1) * SEL, 0:SC],
                            qT[half, r, 0, d, g * GROUP:(g + 1) * GROUP, :].rearrange("k t h -> k (t h)"),
                            kT[half, k % 2, g * P:(g + 1) * P], start=True, stop=True)
                last.then_inc(R["score"], 1)

            def turn(n, d):
                k = n * ND + d
                pe.wait_ge(R["prob_n"], k + 1)
                if k:
                    pe.wait_ge(R["prT_done"], k)
                for q in range(2):
                    nc.tensor.transpose(ps_tp[:, q * P:(q + 1) * P], pr[:, k % 2, q, 0:SC], ident)
                    last = nc.tensor.transpose(ps_tp[0:WIN, (2 + q) * P:(3 + q) * P], pr[:, k % 2, q, SC:SW], ident)
                last.then_inc(R["prT_p"], 1)

            def value(n, d):
                r, k = n % RING, n * ND + d
                pe.wait_ge(R["prT_done"], k + 1)
                pe.wait_ge(R["cwin_done"], n + 1)
                pe.wait_ge(R["smax"], min(k + 2, ND * TILES))
                if k == ND * TILES - 1:
                    pe.wait_ge(R["o_done"], k)
                for q in range(2):
                    for part in range(2):
                        for g in range(GROUP):
                            queries = slice(g * GROUP, (g + 1) * GROUP)
                            o = OUT + g * GROUP * NH
                            if part == 0:
                                keys, weights = c_win[:, r, 2 * d + q, :], prTw[:, k % 2, q, queries, :]
                            else:
                                keys = gath[:, r, slot(2 * GROUP * d + GROUP * q + g), 0:DC]
                                weights = prT[:, k % 2, q, queries, :]
                            last = nc.tensor.matmul(ps_s[q][g * DC:(g + 1) * DC, o:o + GROUP * NH], keys,
                                                    weights.rearrange("s t h -> s (t h)"),
                                                    start=(part == 0), stop=(part == 1), skip_group_check=True)
                last.then_inc(R["value"], 1)

            def mix(n):
                pe.wait_ge(R["o_done"], ND * (n + 1))
                if n + AHEAD1 - BEHIND < TILES:
                    pe.wait_ge(R["x1"], n + AHEAD1 - BEHIND + 1)
                else:
                    pe.wait_ge(R["x1"], TILES)
                    pe.wait_ge(R["x3"], n)
                for h in range(NH):
                    last = nc.tensor.matmul(ps_f2[:, HID:512], oT[:, n % 2, :, h], wvo[:, h, :], start=(h == 0), stop=(h == NH - 1))
                last.then_inc(R["x2_y"], 1)

            run_parts("PE", {"norm1": turned("1"), "gate1": lambda n: gate_up("1", n), "hid1": lambda n: down("1", n),
                       "normm": turned("m"), "proj": proj, **{f"index{j}": index(j) for j in range(4)}, "query": query, "keysT": keys_turned,
                       "cwin": cwin, "queryT0": queryT(0), "queryT1": queryT(1), "key": key, "score": score, "turn": turn, "value": value,
                       "mix": mix, "norm2": turned("2"), "gate2": lambda n: gate_up("2", n),
                       "hid2": lambda n: down("2", n)},
                      {"gate1": setup_products, "index3": setup_query})


_INS = ['L0_attn_x', 'L0_attn_W_dkv', 'L0_attn_W_uk', 'L0_attn_W_uv', 'L0_attn_W_dq', 'L0_attn_W_uq', 'L0_attn_W_qr',
        'L0_attn_W_kr', 'L0_attn_W_out', 'L0_attn_idx_wq', 'L0_attn_idx_wk', 'L0_attn_idx_w', 'L0_attn_raw_delta',
        'L0_ffn_w_gate', 'L0_ffn_w_up', 'L0_ffn_w_down']


def kernel(**inputs):
    import concourse.bacc as _bacc
    from concourse.bass_utils import run_bass_kernel_spmd as _run

    nc = _bacc.Bacc("TRN2", target_bir_lowering=False, num_devices=1)
    arrays, args = {}, []
    for name in _INS + ["shape_constants"]:
        a = shape_constants() if name == "shape_constants" else np.ascontiguousarray(inputs[name])
        arrays[f"in_{name}"] = a
        args.append(nc.dram_tensor(f"in_{name}", a.shape, mybir.dt.from_np(a.dtype), kind="ExternalInput").ap())
    out = nc.dram_tensor("out_0", (BATCH, LEN, D), F32, kind="ExternalOutput").ap()
    macaron_block(nc, *args, out)
    r = _run(nc, [arrays], core_ids=[0])
    return r.results[0]["out_0"]
```
